# Optimizing a Trainium2 kernel written in Bass

```python
import numpy as np
import jax
import jax.numpy as jnp

def _softmax(x, axis=-1):
    return jax.nn.softmax(x, axis=axis)
def _gelu(x):
    return jax.nn.gelu(x, approximate=True)
def _silu(x):
    return jax.nn.silu(x)
def _sigmoid(x):
    return jax.nn.sigmoid(x)
def _layernorm(x, axis=-1, eps=1e-5):
    m = jnp.mean(x, axis=axis, keepdims=True)
    v = jnp.var(x, axis=axis, keepdims=True)
    return (x - m) / jnp.sqrt(v + eps)
def _scatter_add(tgt, idx, src, axis=0):
    return tgt.at[idx].add(src)
def _segment_sum(src, seg, n):
    return jax.ops.segment_sum(src, seg, n)

kernel_name = 'mk_conv_preact_d4_conv_nhwc32_ff3963'

def setup_inputs(seed: int = 0):
    np.random.seed(seed)
    _w = jnp.asarray
    def _rec_inputs():
        import jax
        import jax.numpy as jnp
        _gk = jax.random.key(seed)
        x = 7.22e-05 + 1 * jax.random.normal(jax.random.fold_in(_gk, 1), (64, 64, 64, 32), jnp.float32)
        return x
    x = _rec_inputs()
    def _L0_conv_setup():
        import jax, jax.numpy as jnp
        import numpy as np
        D = H = W = 64
        C_IN = 32
        C_OUT = 32
        M1 = M2 = M3 = 16
        key = jax.random.key(seed)
        ks = jax.random.split(key, 9)
        scale = 1.0 / (C_IN * C_OUT)
        wshape = (C_IN, C_OUT, M1, M2, M3)
        u = lambda k: jax.random.uniform(k, wshape, minval=-scale, maxval=scale, dtype=jnp.float32)
        return {'x': jax.random.normal(ks[0], (D, H, W, C_IN), dtype=jnp.float32), 'w1r': u(ks[1]), 'w1i': u(ks[2]), 'w2r': u(ks[3]), 'w2i': u(ks[4]), 'w3r': u(ks[5]), 'w3i': u(ks[6]), 'w4r': u(ks[7]), 'w4i': u(ks[8])}
    _L0_conv_all = _L0_conv_setup()
    _L0_conv_in = {k: v for k, v in _L0_conv_all.items() if k in ('w1r', 'w1i', 'w2r', 'w2i', 'w3r', 'w3i', 'w4r', 'w4i', )}
    del _L0_conv_all

    def _L1_conv_setup():
        import jax, jax.numpy as jnp
        import numpy as np
        GRID_SIZE = 5
        SPLINE_ORDER = 3
        GRID_RANGE = (-1.0, 1.0)
        NUM_BASIS = GRID_SIZE + SPLINE_ORDER

        def _spline_bases(x, grid, spline_order):
            xg = x[..., None]
            bases = ((xg >= grid[:-1]) & (xg < grid[1:])).astype(x.dtype)
            for k in range(1, spline_order + 1):
                left = (xg - grid[:-(k + 1)]) / (grid[k:-1] - grid[:-(k + 1)]) * bases[..., :-1]
                right = (grid[k + 1:] - xg) / (grid[k + 1:] - grid[1:-k]) * bases[..., 1:]
                bases = left + right
            return bases
        key = jax.random.key(seed)
        k1, k2 = jax.random.split(key)
        x = jax.random.normal(k1, (16, 256, 256, 32), dtype=jnp.float32)
        bound = GRID_RANGE[1] - GRID_RANGE[0]
        grid = jnp.linspace(GRID_RANGE[0] - SPLINE_ORDER * bound / GRID_SIZE, GRID_RANGE[1] + SPLINE_ORDER * bound / GRID_SIZE, GRID_SIZE + 2 * SPLINE_ORDER + 1).astype(jnp.float32)
        W = jax.random.normal(k2, (32, NUM_BASIS), dtype=jnp.float32) * 0.1
        return {'x': x, 'grid': grid, 'W': W}
    _L1_conv_all = _L1_conv_setup()
    _L1_conv_in = {k: v for k, v in _L1_conv_all.items() if k in ('grid', 'W', )}
    del _L1_conv_all

    def _L2_conv_setup():
        import jax, jax.numpy as jnp
        from jax import lax
        import numpy as np

        @jax.custom_vjp
        def ste_sign(x):
            return jnp.where(x >= 0, 1.0, -1.0).astype(x.dtype)

        def _ste_fwd(x):
            return (ste_sign(x), x)

        def _ste_bwd(x, g):
            return (g * (jnp.abs(x) <= 1.0).astype(g.dtype),)
        ste_sign.defvjp(_ste_fwd, _ste_bwd)
        key = jax.random.key(seed)
        k1, k2 = jax.random.split(key)
        B, H, Wd, Cin = (16, 256, 256, 32)
        M, kh, kw, Cout = (4, 3, 3, 32)
        x = jax.random.normal(k1, (B, H, Wd, Cin), dtype=jnp.float32)
        W = jax.random.normal(k2, (M, kh, kw, Cin, Cout), dtype=jnp.float32)
        b = jnp.zeros((M, Cout), dtype=jnp.float32)
        return {'x': x, 'W': W, 'b': b}
    _L2_conv_all = _L2_conv_setup()
    _L2_conv_in = {k: v for k, v in _L2_conv_all.items() if k in ('W', 'b', )}
    del _L2_conv_all

    def _L3_conv_setup():
        import jax, jax.numpy as jnp
        import numpy as np
        B, H, Wd, C = (8, 512, 512, 32)
        MODES = 32
        key = jax.random.key(seed)
        k1, k2 = jax.random.split(key)
        x = jax.random.normal(k1, (B, H, Wd, C), dtype=jnp.float32)
        scale = (2.0 / (C + C)) ** 0.5
        W = jax.random.normal(k2, (MODES, MODES, C, C), dtype=jnp.float32) * scale
        return {'x': x, 'W': W}
    _L3_conv_all = _L3_conv_setup()
    _L3_conv_in = {k: v for k, v in _L3_conv_all.items() if k in ('W', )}
    del _L3_conv_all

    return {
        "x": x,
        "L0_conv_w1r": _L0_conv_in["w1r"],
        "L0_conv_w1i": _L0_conv_in["w1i"],
        "L0_conv_w2r": _L0_conv_in["w2r"],
        "L0_conv_w2i": _L0_conv_in["w2i"],
        "L0_conv_w3r": _L0_conv_in["w3r"],
        "L0_conv_w3i": _L0_conv_in["w3i"],
        "L0_conv_w4r": _L0_conv_in["w4r"],
        "L0_conv_w4i": _L0_conv_in["w4i"],
        "L1_conv_grid": _L1_conv_in["grid"],
        "L1_conv_W": _L1_conv_in["W"],
        "L2_conv_W": _L2_conv_in["W"],
        "L2_conv_b": _L2_conv_in["b"],
        "L3_conv_W": _L3_conv_in["W"],
    }

def reference(x, L0_conv_w1r, L0_conv_w1i, L0_conv_w2r, L0_conv_w2i, L0_conv_w3r, L0_conv_w3i, L0_conv_w4r, L0_conv_w4i, L1_conv_grid, L1_conv_W, L2_conv_W, L2_conv_b, L3_conv_W):
    import jax
    import jax.numpy as jnp
    def _L0_conv_ref(x, w1r, w1i, w2r, w2i, w3r, w3i, w4r, w4i):
        import jax, jax.numpy as jnp
        import numpy as np
        D = H = W = 64
        C_IN = 32
        C_OUT = 32
        M1 = M2 = M3 = 16
        d, h, w, c = x.shape
        fft_d, fft_h, fft_w = (2 * d - 1, 2 * h - 1, 2 * w - 1)
        X = jnp.fft.rfftn(x, s=(fft_d, fft_h, fft_w), axes=(0, 1, 2), norm='ortho')
        freq_d, freq_h, freq_w = (X.shape[0], X.shape[1], X.shape[2])
        w1 = w1r + 1j * w1i
        w2 = w2r + 1j * w2i
        w3 = w3r + 1j * w3i
        w4 = w4r + 1j * w4i
        m1 = min(w1r.shape[2], (freq_d + 1) // 2)
        m2 = min(w1r.shape[3], (freq_h + 1) // 2)
        m3 = min(w1r.shape[4], freq_w)
        w1s = w1[:, :, :m1, :m2, :m3]
        w2s = w2[:, :, :m1, :m2, :m3]
        w3s = w3[:, :, :m1, :m2, :m3]
        w4s = w4[:, :, :m1, :m2, :m3]
        oc1 = jnp.einsum('dhwi,iodhw->dhwo', X[:m1, :m2, :m3, :], w1s)
        oc2 = jnp.einsum('dhwi,iodhw->dhwo', X[:m1, -m2:, :m3, :], w2s)
        oc3 = jnp.einsum('dhwi,iodhw->dhwo', X[-m1:, :m2, :m3, :], w3s)
        oc4 = jnp.einsum('dhwi,iodhw->dhwo', X[-m1:, -m2:, :m3, :], w4s)
        out_ft = jnp.zeros((freq_d, freq_h, freq_w, w1r.shape[1]), dtype=jnp.complex64)
        out_ft = out_ft.at[:m1, :m2, :m3, :].set(oc1)
        out_ft = out_ft.at[:m1, -m2:, :m3, :].set(oc2)
        out_ft = out_ft.at[-m1:, :m2, :m3, :].set(oc3)
        out_ft = out_ft.at[-m1:, -m2:, :m3, :].set(oc4)
        y = jnp.fft.irfftn(out_ft, s=(fft_d, fft_h, fft_w), axes=(0, 1, 2), norm='ortho')
        return y[:d, :h, :w, :]

    def _L1_conv_ref(x, grid, W):
        import jax, jax.numpy as jnp
        import numpy as np
        GRID_SIZE = 5
        SPLINE_ORDER = 3
        GRID_RANGE = (-1.0, 1.0)
        NUM_BASIS = GRID_SIZE + SPLINE_ORDER

        def _spline_bases(x, grid, spline_order):
            xg = x[..., None]
            bases = ((xg >= grid[:-1]) & (xg < grid[1:])).astype(x.dtype)
            for k in range(1, spline_order + 1):
                left = (xg - grid[:-(k + 1)]) / (grid[k:-1] - grid[:-(k + 1)]) * bases[..., :-1]
                right = (grid[k + 1:] - xg) / (grid[k + 1:] - grid[1:-k]) * bases[..., 1:]
                bases = left + right
            return bases
        bases = _spline_bases(x, grid, SPLINE_ORDER)
        return jnp.einsum('...ck,ck->...c', bases, W)

    def _L2_conv_ref(x, W, b):
        import jax, jax.numpy as jnp
        from jax import lax
        import numpy as np

        @jax.custom_vjp
        def ste_sign(x):
            return jnp.where(x >= 0, 1.0, -1.0).astype(x.dtype)

        def _ste_fwd(x):
            return (ste_sign(x), x)

        def _ste_bwd(x, g):
            return (g * (jnp.abs(x) <= 1.0).astype(g.dtype),)
        ste_sign.defvjp(_ste_fwd, _ste_bwd)
        xq = ste_sign(x)
        wq = ste_sign(W)
        w_sum = wq.sum(axis=0)
        y = lax.conv_general_dilated(xq, w_sum, window_strides=(1, 1), padding='SAME', dimension_numbers=('NHWC', 'HWIO', 'NHWC'))
        return y + b.sum(axis=0)

    def _L3_conv_ref(x, W):
        import jax, jax.numpy as jnp
        import numpy as np
        B, H, Wd, C = (8, 512, 512, 32)
        MODES = 32
        modes = W.shape[0]
        h, w = (x.shape[1], x.shape[2])
        xf = jnp.fft.rfft2(x, axes=(1, 2))
        low = xf[:, :modes, :modes, :]
        out_low = jnp.einsum('bxyc,xycd->bxyd', low, W.astype(xf.dtype))
        out_f = jnp.pad(out_low, ((0, 0), (0, xf.shape[1] - modes), (0, xf.shape[2] - modes), (0, 0)))
        return jnp.fft.irfft2(out_f, s=(h, w), axes=(1, 2))

    def _gn(v, G=16, eps=1e-5):
        B_, H_, W_, C_ = v.shape
        g = v.reshape(B_, H_, W_, G, C_ // G)
        m = jnp.mean(g, axis=(1, 2, 4), keepdims=True)
        s = jnp.var(g, axis=(1, 2, 4), keepdims=True)
        return ((g - m) / jnp.sqrt(s + eps)).reshape(v.shape)

    def _ln_c(v, eps=1e-6):
        m = jnp.mean(v, axis=-1, keepdims=True)
        s = jnp.var(v, axis=-1, keepdims=True)
        return (v - m) / jnp.sqrt(s + eps)

    def _ln_t(v, eps=1e-5):
        m = jnp.mean(v, axis=-1, keepdims=True)
        s = jnp.var(v, axis=-1, keepdims=True)
        return (v - m) / jnp.sqrt(s + eps)

    def _to_tokens(v):
        B_, H_, W_, C_ = v.shape
        return v.reshape(B_, H_ * W_, C_)
    def _from_tokens(t, like):
        return t.reshape(like.shape)

    x = x + _L0_conv_ref(_gn(x), L0_conv_w1r, L0_conv_w1i, L0_conv_w2r, L0_conv_w2i, L0_conv_w3r, L0_conv_w3i, L0_conv_w4r, L0_conv_w4i)
    x = x + _L1_conv_ref(_gn(x), L1_conv_grid, L1_conv_W)
    x = x + _L2_conv_ref(_gn(x), L2_conv_W, L2_conv_b)
    x = x + _L3_conv_ref(_gn(x), L3_conv_W)
    return x


_drawn_inputs = setup_inputs


def setup_inputs(seed=0):
    import zlib

    import numpy as np

    out = dict(_drawn_inputs(seed))
    spreads = {'L2_conv_b': (0.0, 0.8)}
    factors = {'L0_conv_w1r': 19.075,
     'L0_conv_w1i': 19.951,
     'L0_conv_w2r': 19.535,
     'L0_conv_w2i': 7.508,
     'L0_conv_w3r': 7.283,
     'L0_conv_w3i': 19.463,
     'L0_conv_w4r': 19.106,
     'L0_conv_w4i': 19.271,
     'L3_conv_W': 2.73}
    for name, (base, spread) in spreads.items():
        noise = np.random.default_rng([zlib.crc32(name.encode()), seed]).standard_normal(out[name].shape)
        drawn = base * np.exp(spread * noise) if base else spread * noise
        out[name] = jnp.asarray(drawn.astype(out[name].dtype))
    for name, factor in factors.items():
        out[name] = (out[name] * factor).astype(out[name].dtype)
    return out
```

```python
from contextlib import ExitStack

import concourse.bass as bass
from concourse import mybir

F32 = mybir.dt.float32
BF16 = mybir.dt.bfloat16
ALU = mybir.AluOpType
ACT = mybir.ActivationFunctionType
AX_X = mybir.AxisListType.X

D = H = W = 64
C = 32
G = 16
PAIR = 2
NP = D // PAIR
M = 16
KH = 2 * M
KW = M
M3 = 32
KNOTS, BASES, ORDER = 12, 8, 3
LEFT, RIGHT = range(1, 6), range(6, 11)
MID = 5
EPS = 1e-5
ROW = W * C


def later(i):
    return not isinstance(i, int) or i >= 2


def steps(eng, n, body, peel=2):
    for i in range(peel):
        body(i, i % 2, i // 2)
    with eng.Fori(peel // 2, n // 2 - 1) as j:
        body(2 * j, 0, j)
        body(2 * j + 1, 1, j)
    body(n - 2, 0, n // 2 - 1)
    body(n - 1, 1, n // 2 - 1)


class Places:

    def __init__(self, nc, ctx, tag):
        self.nc, self.ctx, self.tag = nc, ctx, tag

    def sb(self, name, shape, dt=F32):
        return self.ctx.enter_context(self.nc.sbuf_tensor(f"{self.tag}_{name}", shape, dt))

    def ps(self, name, cols=512):
        return self.ctx.enter_context(self.nc.psum_tensor(f"{self.tag}_{name}", [128, cols], F32))

    def sem(self, name):
        return self.ctx.enter_context(self.nc.semaphore(f"{self.tag}_{name}"))


class RowStats:

    def __init__(self, pl, psum):
        self.bn = pl.sb("bn", [128, G, 6])
        self.ms = pl.sb("ms", [128, G])
        self.mu = pl.sb("mu", [128, G])
        self.dev = pl.sb("dev", [128, G, 2])
        self.dev2 = pl.sb("dev2", [128, G, 2])
        self.sq = pl.sb("sq", [128, G, 2])
        self.vr = pl.sb("vr", [128, PAIR, G])
        self.ve = [pl.sb(f"ve{p}", [128, PAIR, G]) for p in range(2)]
        self.rstd = [pl.sb(f"rstd{p}", [128, PAIR, G]) for p in range(2)]
        self.mhalf = pl.sb("mhalf", [128, PAIR, G])
        self.avg = pl.sb("avg", [128, 128])
        self.var = pl.sb("var", [128, PAIR, 128])
        self.pm = psum[:, 0:G]
        self.pv = psum[:, 64:64 + PAIR * G * 2]
        self.s_bn = pl.sem("s_bn")
        self.s_ms = pl.sem("s_ms")
        self.s_pm = pl.sem("s_pm")
        self.s_mu = pl.sem("s_mu")
        self.s_dev = pl.sem("s_dev")
        self.s_dev2 = pl.sem("s_dev2")
        self.s_sq = pl.sem("s_sq")
        self.s_pv = pl.sem("s_pv")
        self.s_vr = pl.sem("s_vr")
        self.s_ve = pl.sem("s_ve")
        self.s_rstd = pl.sem("s_rstd")
        self.s_xn = pl.sem("s_xn")
        self.s_mh = pl.sem("s_mh")


def center(eng, st, mean, x, out):
    eng.tensor_tensor(out.rearrange("p (g c w) -> p g c w", g=G, c=2),
                      x.rearrange("p (w g c) -> p g c w", g=G, c=2),
                      mean.unsqueeze(2).unsqueeze(3).broadcast_to([128, G, 2, W]),
                      ALU.subtract).then_inc(st.s_xn, 1)


def row_stats_start(dve, st, i, x):
    xg = x.rearrange("p (w g c) -> p g w c", g=G, c=2)
    for g in range(G):
        ins = dve.bn_stats(st.bn[:, g, :], xg[:, g])
    ins.then_inc(st.s_bn, 1)
    dve.wait_ge(st.s_bn, i + 1)
    dve.tensor_tensor(st.ms[:, :], st.bn[:, :, 1], st.bn[:, :, 4], ALU.add).then_inc(st.s_ms, 1)


def row_stats_middle(dve, st, i):
    dve.wait_ge(st.s_pm, i + 1)
    if not (isinstance(i, int) and i == 0):
        dve.wait_ge(st.s_xn, i)
    dve.tensor_copy(st.mu[:, :], st.pm).then_inc(st.s_mu, 1)
    dve.tensor_tensor(st.dev[:, :, :], st.bn[:, :, 1::3], st.pm.unsqueeze(2).broadcast_to([128, G, 2]),
                      ALU.subtract).then_inc(st.s_dev, 1)
    dve.wait_ge(st.s_dev, i + 1)
    dve.scalar_tensor_tensor(st.dev2[:, :, :], st.dev[:, :, :], float(W), st.dev[:, :, :],
                             ALU.mult, ALU.mult).then_inc(st.s_dev2, 1)
    dve.wait_ge(st.s_dev2, i + 1)
    dve.tensor_tensor(st.sq[:, :, :], st.dev2[:, :, :], st.bn[:, :, 2::3], ALU.add).then_inc(st.s_sq, 1)


def row_stats_end(dve, st, i, p):
    dve.wait_ge(st.s_pv, i + 1)
    dve.tensor_reduce(st.vr[:, :, :], st.pv.rearrange("p (d g c) -> p d g c", d=PAIR, c=2), AX_X,
                      ALU.add).then_inc(st.s_vr, 1)
    if later(i):
        dve.wait_ge(st.s_rstd, i - 1)
    dve.wait_ge(st.s_vr, i + 1)
    dve.tensor_scalar(st.ve[p][:, :, :], st.vr[:, :, :], EPS, None, ALU.add).then_inc(st.s_ve, 1)


def row_mean_tensor(pe, st, i):
    pe.wait_ge(st.s_ms, i + 1)
    pe.matmul(st.pm, st.avg[:, :], st.ms[:, :], start=True, stop=True).then_inc(st.s_pm, 1)


def row_variance_tensor(pe, st, i):
    pe.wait_ge(st.s_sq, i + 1)
    for d2 in range(PAIR):
        ins = pe.matmul(st.pv[:, d2 * 32:d2 * 32 + 32], st.var[:, d2, :],
                        st.sq[:, :, :].rearrange("p g c -> p (g c)"), start=True, stop=True)
    ins.then_inc(st.s_pv, 1)


def row_stats_root(pool, st, i, p):
    pool.wait_ge(st.s_ve, i + 1)
    pool.tensor_tensor(st.rstd[p][:, :, :], st.ve[p][:, :, :], st.mhalf[:, :, :], ALU.pow).then_inc(st.s_rstd, 1)


def phase_forward(nc, x, consts, spectra_dram):
    with ExitStack() as ctx:
        pl = Places(nc, ctx, "A")
        X = [pl.sb(f"x{p}", [128, ROW]) for p in range(2)]
        XN = [pl.sb(f"xn{p}", [128, ROW]) for p in range(2)]
        hw = [pl.sb(f"rows{p}", [128, 4 * 512]) for p in range(2)]
        Z = [pl.sb(f"z{p}", [128, PAIR, KH, 8]) for p in range(2)]
        fh = pl.sb("fh", [128, 128])
        fw = pl.sb("fw", [128, 2, 64])
        P_h = [pl.ps(f"ph{b}") for b in range(4)]
        P_z = [pl.ps(f"pz{b}") for b in range(2)]
        P_s = pl.ps("pstat")
        st = RowStats(pl, P_s)
        s_const = pl.sem("const")
        x_in = [pl.sem(f"x_in{p}") for p in range(2)]
        z_out = [pl.sem(f"z_out{p}") for p in range(2)]
        s_h = pl.sem("h")
        s_rows = pl.sem("rows")
        s_w = pl.sem("w")
        s_z = pl.sem("z")
        xv = x.rearrange("(n d) h w c -> n h d (w c)", d=PAIR)
        block = ctx.enter_context(nc.Block())

        @block.sync
        def _(sp):
            for dst, name in ((fh, "fh0"), (fw, "fw0"), (st.avg, "avg"), (st.var, "var")):
                sp.dma_start(dst[:], consts[name]).then_inc(s_const, 16)

            def load(i, p, j):
                if later(i):
                    sp.wait_ge(st.s_xn, i - 1)
                sp.dma_start(X[p][:, :], xv[i]).then_inc(x_in[p], 16)

            steps(sp, NP, load)

        @block.scalar
        def _(act):
            def step(i, p, j):
                for b in range(4):
                    act.wait_ge(s_h, 4 * i + b + 1)
                    if b == 0 and later(i):
                        act.wait_ge(s_w, i - 1)
                    act.activation(hw[p][:, b * 512:(b + 1) * 512], P_h[b][:, :], ACT.Copy).then_inc(s_rows, 1)
                act.wait_ge(s_z, 2 * i + 2)
                for half in range(2):
                    for ri in range(2):
                        lo = half * 64 + ri * 32
                        act.dma_start(spectra_dram[ri, bass.ds(i * PAIR, PAIR), half].rearrange("d k f -> k d f"),
                                      Z[p][lo:lo + 32].rearrange("k d h g -> k d (h g)")).then_inc(z_out[p], 16)

            steps(act, NP, step)
            for p in range(2):
                act.wait_ge(z_out[p], 64 * (NP // 2))

        @block.gpsimd
        def _(pool):
            pool.memset(st.mhalf[:, :, :], -0.5).then_inc(st.s_mh, 1)
            pool.wait_ge(st.s_mh, 1)

            def root(i, p, j):
                if later(i):
                    pool.wait_ge(s_z, 2 * (i - 1))
                row_stats_root(pool, st, i, p)

            steps(pool, NP, root)

        @block.vector
        def _(dve):
            def stats(i, p, j):
                dve.wait_ge(x_in[p], 16 * (j + 1))
                row_stats_start(dve, st, i, X[p][:, :])
                row_stats_middle(dve, st, i)
                if later(i):
                    dve.wait_ge(s_h, 4 * (i - 1))
                dve.wait_ge(st.s_mu, i + 1)
                center(dve, st, st.mu[:, :], X[p][:, :], XN[p][:, :])
                row_stats_end(dve, st, i, p)

            def step(i, p, j):
                if not (isinstance(i, int) and i == NP - 1):
                    stats(i + 1, 1 - p, j + p)
                dve.wait_ge(s_w, i + 1)
                dve.wait_ge(st.s_rstd, i + 1)
                if later(i):
                    dve.wait_ge(z_out[p], 64 * j)
                for half in range(2):
                    rows = slice(half * 64, half * 64 + 64)
                    ins = dve.tensor_tensor(
                        Z[p][rows].rearrange("p d h g -> p g d h"),
                        P_z[p][rows].rearrange("p (g d h) -> p g d h", g=8, d=PAIR),
                        st.rstd[p][rows, :, half * 8:half * 8 + 8].rearrange("p d g -> p g d").unsqueeze(3)
                        .broadcast_to([64, 8, PAIR, KH]), ALU.mult)
                    ins.then_inc(s_z, 1)

            stats(0, 0, 0)
            steps(dve, NP, step)

        @block.tensor
        def _(pe):
            pe.wait_ge(s_const, 64)

            def step(i, p, j):
                more = not (isinstance(i, int) and i == NP - 1)
                pe.wait_ge(st.s_xn, i + 1)
                for g in range(G):
                    if g % 4 == 0 and not (isinstance(i, int) and i == 0):
                        pe.wait_ge(s_rows, 4 * (i - 1) + g // 4 + 1)
                    ins = pe.matmul(P_h[g // 4][:, g % 4 * 128:g % 4 * 128 + 128], XN[p][:, g * 128:g * 128 + 128], fh[:, :],
                                    start=True, stop=True)
                    if g % 4 == 3:
                        ins.then_inc(s_h, 1)
                if more:
                    row_mean_tensor(pe, st, i + 1)
                pe.wait_ge(s_rows, 4 * i + 4)
                if later(i):
                    pe.wait_ge(s_z, 2 * (i - 1))
                hv = hw[p][:, :].rearrange("p (g r n) -> p r g n", g=G, r=2)
                for ri in range(2):
                    for half in range(2):
                        ins = pe.matmul(P_z[p][half * 64:half * 64 + 64, :], fw[:, ri, :],
                                        hv[:, ri, half * 8:half * 8 + 8], start=(ri == 0), stop=(ri == 1))
                ins.then_inc(s_w, 1)
                if more:
                    row_variance_tensor(pe, st, i + 1)

            row_mean_tensor(pe, st, 0)
            row_variance_tensor(pe, st, 0)
            steps(pe, NP, step)


def phase_depth(nc, consts, spectra_dram, weights, modes_dram, images_dram):
    with ExitStack() as outer:
        S = outer.enter_context(nc.sbuf_tensor("B_modes", [128, 32, 512], F32))

        with ExitStack() as ctx:
            pl = Places(nc, ctx, "B1")
            D1 = pl.sb("d1", [128, 4, KW, 256])
            T = [pl.sb(f"t{p}", [128, KH, C]) for p in range(2)]
            fd = pl.sb("fd", [128, 4, 32])
            P = [[pl.ps(f"p{p}{hh}") for hh in range(2)] for p in range(2)]
            s_in = pl.sem("in")
            s_t = [pl.sem(f"t{c}") for c in range(2)]
            s_f = pl.sem("f")
            s_s = [pl.sem(f"s{hh}") for hh in range(2)]
            block = ctx.enter_context(nc.Block())

            def lay_out(copy, eng, c2, i, p, j):
                if later(i):
                    eng.wait_ge(s_f, 2 * (i - 1))
                src = D1[:].rearrange("q (a c) k (h g) -> q c k a h g", c=2, g=8)[:, c2]
                src = src[:, i if isinstance(i, int) else bass.ds(i, 1)]
                if not isinstance(i, int):
                    src = src.rearrange("q o a h g -> q (o a) h g")
                dst = T[p][:].rearrange("q h (a g c) -> q c a h g", a=2, g=8)[:, c2]
                copy(dst, src).then_inc(s_t[c2], 1)

            def keep(copy, eng, hh, i, p, j):
                eng.wait_ge(s_f, 2 * i + hh + 1)
                dst = S[:, hh * 16:hh * 16 + 16, :].rearrange("q t (m a r b) -> q a b m t r", m=M, a=2, r=2)[:, p]
                dst = dst[:, j if isinstance(j, int) else bass.ds(j, 1)]
                if not isinstance(j, int):
                    dst = dst.rearrange("q o m t r -> q (o m) t r")
                src = P[p][hh][:, :].rearrange("q (m t r) -> q m t r", m=M, r=2)
                copy(dst, src).then_inc(s_s[hh], 1)

            @block.sync
            def _(sp):
                sp.dma_start(fd[:], consts["fd0"].rearrange("p (r f) -> p r f", r=4)).then_inc(s_in, 16)
                src = spectra_dram.rearrange("r d h (c k) f -> (r d) (h c) k f", c=2)
                for a in range(4):
                    sp.dma_start(D1[:, a], src[:, a]).then_inc(s_in, 16)

            def copier(eng, copy, share):
                eng.wait_ge(s_in, 80)
                lay_out(copy, eng, share, 0, 0, 0)

                def step(i, p, j):
                    if not (isinstance(i, int) and i == KW - 1):
                        lay_out(copy, eng, share, i + 1, 1 - p, j + p)
                    keep(copy, eng, share, i, p, j)

                steps(eng, KW, step)

            @block.scalar
            def _(act):
                copier(act, lambda d, s: act.activation(d, s, ACT.Copy), 0)

            @block.vector
            def _(dve):
                copier(dve, lambda d, s: dve.tensor_copy(d, s), 1)

            @block.tensor
            def _(pe):
                pe.wait_ge(s_in, 80)

                def step(i, p, j):
                    for c2 in range(2):
                        pe.wait_ge(s_t[c2], i + 1)
                    for kh in range(KH):
                        hh, m2 = divmod(kh, M)
                        if m2 == 0 and later(i):
                            pe.wait_ge(s_s[hh], i - 1)
                        for rows in range(4):
                            q, role = divmod(rows, 2)
                            ins = pe.matmul(P[p][hh][rows * 32:rows * 32 + 32, m2 * 32:m2 * 32 + 32],
                                            T[p][:, kh, :], fd[:, role * 2 + q, :], start=True, stop=True)
                        if m2 == M - 1:
                            ins.then_inc(s_f, 1)

                steps(pe, KW, step)

        with ExitStack() as ctx:
            pl = Places(nc, ctx, "B2")
            WT = [pl.sb(f"w{p}", [128, C, M * M]) for p in range(2)]
            SZ = [pl.sb(f"sz{p}", [128, 32, 32]) for p in range(2)]
            cross = pl.sb("cross", [128, 64 * C])
            R = [pl.sb(f"r{p}", [128, 8 * C]) for p in range(2)]
            diag = pl.sb("diag", [128, 8])
            P = [pl.ps(f"p{p}", 4 * 512) for p in range(2)]
            s_const = pl.sem("const")
            s_zero = pl.sem("zero")
            w_in = [pl.sem(f"w_in{p}") for p in range(2)]
            r_out = [pl.sem(f"r_out{p}") for p in range(2)]
            s_sz = pl.sem("sz")
            s_mm = pl.sem("mm")
            s_cross = pl.sem("cross")
            s_r = pl.sem("r")
            block = ctx.enter_context(nc.Block())
            TILES = 32

            def tiles(eng, body):
                for corner in range(4):
                    for p in range(2):
                        if corner == 0:
                            body(p, p, 0, corner, p)
                        else:
                            body(8 * corner + p, p, 4 * corner, corner, p)
                    with eng.Fori(1, 4) as j:
                        for p in range(2):
                            body(2 * j + (8 * corner + p), p, j + 4 * corner, corner, 2 * j + p)

            @block.sync
            def _(sp):
                sp.dma_start(diag[:], consts["diag8"]).then_inc(s_const, 16)

                def load(i, p, j, corner, m1):
                    if later(i):
                        sp.wait_ge(s_mm, i - 1)
                    hh, dh = divmod(corner, 2)
                    for q in range(2):
                        for part in range(2):
                            w = weights[dh * 2 + hh][part]
                            lo = q * 64 + part * 32
                            sp.dma_start(WT[p][lo:lo + 32],
                                         w.rearrange("i o a b c -> i a o (b c)")[:, m1 + 8 * q]
                                         if isinstance(m1, int) else
                                         w.rearrange("i o a b c -> i a o (b c)")[:, bass.ds(m1 + 8 * q, 1)]
                                         .rearrange("i x o f -> i (x o) f")).then_inc(w_in[p], 16)

                tiles(sp, load)

            @block.scalar
            def _(act):
                act.wait_ge(s_zero, 2)

                def step(i, p, j, corner, m1):
                    if later(i):
                        act.wait_ge(s_mm, i - 1)
                    t = i
                    for q in range(2):
                        rows = slice(q * 64, q * 64 + 64)
                        src = S[rows, t] if isinstance(t, int) else S[rows, bass.ds(t, 1)].rearrange("q o f -> q (o f)")
                        act.activation(SZ[p][rows, :, q * 16:q * 16 + 16], src.rearrange("q (m f) -> q m f", f=16),
                                       ACT.Copy).then_inc(s_sz, 1)

                def out(i, p, j):
                    act.wait_ge(s_r, i + 1)
                    act.dma_start(modes_dram[bass.ds(i, 1)].rearrange("o p f -> (o p) f"), R[p][:]).then_inc(r_out[p], 16)

                step(0, 0, 0, 0, 0)

                def body(i, p, j, corner, m1):
                    if not (isinstance(i, int) and i == TILES - 1):
                        step(i + 1, 1 - p, j + p, corner, m1)
                    out(i, p, j)

                for i in range(2):
                    body(i, i, 0, 0, 0)
                with act.Fori(1, TILES // 2 - 1) as j:
                    body(2 * j, 0, j, 0, 0)
                    body(2 * j + 1, 1, j, 0, 0)
                for i in range(TILES - 2, TILES):
                    body(i, i % 2, i // 2, 0, 0)
                for p in range(2):
                    act.wait_ge(r_out[p], 16 * (TILES // 2))

            @block.gpsimd
            def _(pool):
                for p in range(2):
                    pool.memset(SZ[p][:], 0.0).then_inc(s_zero, 1)

            @block.tensor
            def _(pe):
                pe.wait_ge(s_zero, 2)

                def step(i, p, j):
                    pe.wait_ge(s_sz, 2 * i + 2)
                    pe.wait_ge(w_in[p], 64 * (j + 1))
                    if later(i):
                        pe.wait_ge(s_cross, i - 1)
                    wv = WT[p][:].rearrange("q o (m b a) -> q m a o b", m=M, a=2)
                    for m2 in range(M):
                        for odd in range(2):
                            at = (m2 // 4) * 512 + odd * 256
                            rows = m2 % 4 * 32
                            ins = pe.matmul(P[p][rows:rows + 32, at:at + 256], SZ[p][:, 2 * m2 + odd, :],
                                            wv[:, m2, odd], start=True, stop=True)
                    ins.then_inc(s_mm, 1)

                steps(pe, TILES, step)

            @block.vector
            def _(dve):
                dve.wait_ge(s_const, 16)

                def step(i, p, j):
                    dve.wait_ge(s_mm, i + 1)
                    if not (isinstance(i, int) and i == 0):
                        dve.wait_ge(s_r, i)
                    dve.tensor_tensor(cross[:].rearrange("q (n b) -> q n b", b=8),
                                      P[p][:, :].rearrange("q (n b) -> q n b", b=8),
                                      diag[:].unsqueeze(1).broadcast_to([128, 8 * C, 8]), ALU.mult).then_inc(s_cross, 1)
                    dve.wait_ge(s_cross, i + 1)
                    if later(i):
                        dve.wait_ge(r_out[p], 16 * j)
                    dve.tensor_reduce(R[p][:], cross[:].rearrange("q (n b) -> q n b", b=8), AX_X,
                                      ALU.add).then_inc(s_r, 1)

                steps(dve, TILES, step)

    with ExitStack() as ctx:
        pl = Places(nc, ctx, "B3")
        E1 = pl.sb("e1", [64, 2, 4, 8, 4, 64])
        ed = pl.sb("ed", [64, 128])
        P = [pl.ps(f"p{k}") for k in range(4)]
        Y = [pl.sb(f"y{k}", [128, 512]) for k in range(4)]
        s_in = pl.sem("in")
        s_mm = pl.sem("mm")
        s_y = pl.sem("y")
        y_out = [pl.sem(f"y_out{k}") for k in range(4)]
        block = ctx.enter_context(nc.Block())

        @block.sync
        def _(sp):
            sp.dma_start(ed[:], consts["ed0"]).then_inc(s_in, 16)
            src = modes_dram.rearrange("(hh dh m) (g q r b) f -> r dh q hh m g (b f)", hh=2, dh=2, g=4, q=2, r=2)
            for hh in range(2):
                for rdq in range(8):
                    r, dh, q = rdq // 4, rdq // 2 % 2, rdq % 2
                    lo = r * 32 + dh * 16 + q * 8
                    sp.dma_start(E1[lo:lo + 8, hh].rearrange("k g b m f -> k g (b m f)"),
                                 src[r, dh, q, hh]).then_inc(s_in, 16)
            for kh in range(KH):
                sp.wait_ge(s_y, kh + 1)
                sp.dma_start(images_dram[:, :, kh].rearrange("r d f -> (r d) f"), Y[kh % 4][:]).then_inc(y_out[kh % 4], 16)
            for k in range(4):
                sp.wait_ge(y_out[k], 16 * (KH // 4))

        @block.tensor
        def _(pe):
            pe.wait_ge(s_in, 16 * 17)
            for kh in range(KH):
                hh, m2 = divmod(kh, M)
                if kh >= 4:
                    pe.wait_ge(s_y, kh - 3)
                pe.matmul(P[kh % 4][:, :], ed[:, :], E1[:, hh, m2 % 4, :, m2 // 4, :],
                          start=True, stop=True).then_inc(s_mm, 1)

        @block.scalar
        def _(act):
            for kh in range(KH):
                act.wait_ge(s_mm, kh + 1)
                if kh >= 4:
                    act.wait_ge(y_out[kh % 4], 16 * (kh // 4))
                act.activation(Y[kh % 4][:], P[kh % 4][:, :], ACT.Copy).then_inc(s_y, 1)


def phase_images(nc, x, consts, params, images_dram, x3_dram, spectra3_dram):
    with ExitStack() as ctx:
        pl = Places(nc, ctx, "C")
        grid, spline_w, conv_w, conv_b = params
        KN = [*LEFT, *RIGHT]
        NK = len(KN)
        X = [pl.sb(f"x{p}", [128, ROW]) for p in range(2)]
        IM = [pl.sb(f"im{p}", [64, PAIR, 512]) for p in range(2)]
        AI = pl.sb("ai", [128, 4, 2, 128])
        XT = [pl.sb(f"xt{p}", [128, 16, 128]) for p in range(2)]
        TN = pl.sb("tn", [128, ROW])
        U = pl.sb("u", [128, ROW])
        RK = [pl.sb(f"rk{b}", [128, ROW]) for b in range(2)]
        QK = [pl.sb(f"qk{b}", [128, ROW]) for b in range(2)]
        CK = [pl.sb(f"ck{b}", [128, ROW]) for b in range(2)]
        ACC = pl.sb("acc", [128, ROW])
        SG = pl.sb("sg", [128, 16, (H + 2) * PAIR], BF16)
        X3 = [pl.sb(f"x3{p}", [128, ROW]) for p in range(2)]
        XN3 = pl.sb("xn3", [128, ROW])
        hw = pl.sb("rows", [128, 4 * 512])
        Z = [pl.sb(f"z{p}", [128, G, PAIR * M3]) for p in range(2)]
        gh = pl.sb("gh", [64, 128])
        gw = pl.sb("gw", [128, 2, 512])
        fh = pl.sb("fh", [128, 128])
        fw = pl.sb("fw", [128, 2, 128])
        ident = pl.sb("ident", [128, 128])
        gavg = pl.sb("gavg", [128, 128])
        gsum = pl.sb("gsum", [128, 128])
        WC = pl.sb("wc", [128, 3, 6, C], BF16)
        BT = pl.sb("bt", [128, C])
        gk = pl.sb("gk", [128, KNOTS])
        ngk = pl.sb("ngk", [128, KNOTS])
        coef = pl.sb("coef", [128, KNOTS])
        poly = pl.sb("poly", [128, 4])
        PA = pl.ps("pa", 4 * 512)
        PB = [pl.ps(f"pb{k}") for k in range(3)]
        P_s = pl.ps("pstat")
        st = RowStats(pl, P_s)
        bn1 = pl.sb("bn1", [128, PAIR, 12])
        ms1 = pl.sb("ms1", [128, PAIR])
        vr1 = pl.sb("vr1", [128, PAIR])
        mean1 = pl.sb("mean1", [128, PAIR])
        dv1 = pl.sb("dv1", [128, PAIR, 4])
        dd1 = pl.sb("dd1", [128, PAIR, 4])
        sv1 = pl.sb("sv1", [128, PAIR, 4])
        ve1 = pl.sb("ve_ch", [128, PAIR])
        rstd1 = pl.sb("rs_ch", [128, PAIR])
        sum2 = pl.sb("sum2", [128, PAIR])
        mean2 = pl.sb("mean2", [128, PAIR])
        bias4 = pl.sb("bias4", [128, 4 * C])
        wsp = pl.sb("wsp", [128, BASES])
        w4 = pl.sb("w4", [128, 4 * 9, C])
        wsum = pl.sb("wsum", [128, 9 * C])
        gaps = pl.sb("gaps", [128, KNOTS, KNOTS])
        prod = pl.sb("prod", [128, ORDER + 2, BASES])
        wspan = pl.sb("wspan", [128, BASES])
        shift = pl.sb("shift", [128, MID + 1])
        mom = pl.sb("mom", [128, ORDER + 1, MID + 1])
        msum = pl.sb("msum", [128, ORDER + 1])
        pm1, pv1, pm2 = P_s[:, 160:162], P_s[:, 164:172], P_s[:, 162:164]

        s_const, s_param, s_set = pl.sem("const"), pl.sem("param"), pl.sem("set")
        s_ready0 = pl.sem("ready0")
        x_in = [pl.sem(f"x_in{p}") for p in range(2)]
        im_in = [pl.sem(f"im_in{p}") for p in range(2)]
        x3_out = [pl.sem(f"x3_out{p}") for p in range(2)]
        z_out = [pl.sem(f"z_out{p}") for p in range(2)]
        ring = pl.sem("ring")
        free = [pl.sem(f"free{k}") for k in range(3)]
        s_y = pl.sem("y")
        s_x1 = pl.sem("x1")
        s_bn1, s_ms1, s_vr1, s_pm1, s_mean1 = pl.sem("bn1s"), pl.sem("ms1s"), pl.sem("vr1s"), pl.sem("pm1s"), pl.sem("mean1s")
        s_dv1, s_dd1, s_sv1, s_pv1 = pl.sem("dv1s"), pl.sem("dd1s"), pl.sem("sv1s"), pl.sem("pv1s")
        s_ve1, s_rs1, s_tn, s_clamp = pl.sem("ve1s"), pl.sem("rs1s"), pl.sem("tns"), pl.sem("clamp")
        s_u, s_r, s_q = pl.sem("us"), pl.sem("rs"), pl.sem("qs")
        s_v = pl.sem("v")
        s_cube, s_acc = pl.sem("cube"), pl.sem("accs")
        s_x2, s_pm2, s_mean2, s_sg = pl.sem("x2s"), pl.sem("pm2s"), pl.sem("mean2s"), pl.sem("sgs")
        s_cv = pl.sem("cv")
        s_x3 = pl.sem("x3s")
        s_chain = pl.sem("chain")
        xv = x.rearrange("(n d) h w c -> n h d (w c)", d=PAIR)
        x3v = x3_dram.rearrange("(n d) h f -> n h d f", d=PAIR)
        block = ctx.enter_context(nc.Block())

        def first(i):
            return isinstance(i, int) and i == 0

        def last(i):
            return isinstance(i, int) and i == NP - 1

        def front_use(i, l):
            if first(i):
                return l % 3, l // 3, l + 1
            return l % 3, 4 * i - 2 + l // 3, 12 * i - 5 + l

        def back_use(i, l):
            if last(i):
                return l % 3, 4 * NP - 2 + l // 3, 12 * NP - 5 + l
            return l % 3, 4 * i + 4 + l // 3, 12 * i + 13 + l

        @block.sync
        def _(sp):
            for dst, name in ((gh, "gh0"), (gw, "gw0"), (fh, "fh3"), (fw, "fw3"), (ident, "ident"),
                              (gavg, "gavg"), (gsum, "gsum"), (st.avg, "avg"), (st.var, "var")):
                sp.dma_start(dst[:], consts[name]).then_inc(s_const, 16)

            def load(i, p, j):
                if later(i):
                    sp.wait_ge(ring, front_use(i - 2, 5)[2])
                sp.dma_start(X[p][:, :], xv[i]).then_inc(x_in[p], 16)
                for ri in range(2):
                    sp.dma_start(IM[p][ri * 32:ri * 32 + 32],
                                 images_dram[ri, bass.ds(i * PAIR, PAIR)].rearrange("d k f -> k d f")).then_inc(im_in[p], 16)

            def store_x3(i, p, j):
                sp.wait_ge(s_x3, 4 * i + 4)
                sp.dma_start(x3v[i], X3[p][:, :]).then_inc(x3_out[p], 16)

            def store_z(i, p, j):
                for l in range(2):
                    k, before, use = back_use(i, 4 + l)
                    sp.wait_ge(free[k], before + 1)
                for c2 in range(2):
                    for ri in range(2):
                        lo = c2 * 64 + ri * 32
                        sp.dma_start(spectra3_dram[:, :, c2, ri, bass.ds(i * PAIR * M3, PAIR * M3)],
                                     Z[p][lo:lo + 32]).then_inc(z_out[p], 16)

            load(0, 0, 0)
            load(1, 1, 0)

            def step(i, p, j):
                if not first(i):
                    store_z(i - 1, 1 - p, j)
                if not (isinstance(i, int) and i >= NP - 2):
                    load(i + 2 if isinstance(i, int) else i + 2, p, j + 1)
                store_x3(i, p, j)

            steps(sp, NP, step)
            store_z(NP - 1, 1, 0)
            for p in range(2):
                sp.wait_ge(x3_out[p], 16 * (NP // 2))
                sp.wait_ge(z_out[p], 64 * (NP // 2))

        @block.gpsimd
        def _(pool):
            pool.dma_start(gk[:], grid.rearrange("(o k) -> o k", o=1).broadcast_to([128, KNOTS])).then_inc(s_param, 16)
            pool.dma_start(bias4[:], conv_b.rearrange("m c -> (m c)").rearrange("(o k) -> o k", o=1)
                           .broadcast_to([128, 4 * C])).then_inc(s_param, 16)
            for g in range(4):
                rows = slice(g * C, g * C + C)
                pool.dma_start(wsp[rows], spline_w).then_inc(s_param, 16)
                pool.dma_start(w4[rows], conv_w.rearrange("m a b c o -> c (m a b) o")).then_inc(s_param, 16)
            pool.memset(SG[:], 0.0).then_inc(s_ready0, 1)
            pool.memset(WC[:], 0.0).then_inc(s_ready0, 1)
            pool.memset(st.mhalf[:, :, :], -0.5).then_inc(st.s_mh, 1)
            pool.wait_ge(st.s_mh, 1)

            def root1(i):
                pool.wait_ge(s_ve1, i + 1)
                if not first(i):
                    pool.wait_ge(s_tn, 2 * i)
                pool.tensor_tensor(rstd1[:], ve1[:], st.mhalf[:, 0, 0:PAIR], ALU.pow).then_inc(s_rs1, 1)

            root1(0)

            def step(i, p, j):
                if not last(i):
                    root1(i + 1)
                pool.wait_ge(st.s_mu, i + 1)
                if not first(i):
                    pool.wait_ge(ring, back_use(i - 1, 3)[2])
                center(pool, st, st.mu[:, :], X3[p][:, :], XN3[:, :])
                if later(i):
                    k, before, use = back_use(i - 2, 5)
                    pool.wait_ge(free[k], before + 1)
                row_stats_root(pool, st, i, p)

            steps(pool, NP, step)

        @block.scalar
        def _(act):
            def rows_back(i):
                for l in range(2):
                    k, before, use = front_use(i, l)
                    act.wait_ge(ring, use)
                    if l == 0 and not first(i):
                        act.wait_ge(s_y, i)
                    act.activation(AI[:, 2 * l:2 * l + 2].rearrange("q g r n -> q (g r n)"), PB[k][:, :],
                                   ACT.Copy).then_inc(free[k], 1)

            def turned(i, p, j):
                for l in range(2, 6):
                    k, before, use = front_use(i, l)
                    act.wait_ge(ring, use)
                    if l == 2 and later(i):
                        act.wait_ge(s_cv, 4 * (i - 1))
                    b = l - 2
                    act.activation(XT[p][:, 4 * b:4 * b + 4].rearrange("q w n -> q (w n)"), PB[k][:, :],
                                   ACT.Copy).then_inc(free[k], 1)

            def rows3(i):
                for l in range(4):
                    k, before, use = back_use(i, l)
                    act.wait_ge(ring, use)
                    if l == 0 and not first(i):
                        act.wait_ge(ring, back_use(i - 1, 5)[2])
                    act.activation(hw[:, l * 512:l * 512 + 512], PB[k][:, :], ACT.Copy).then_inc(free[k], 1)

            act.wait_ge(s_set, 1)
            rows_back(0)
            turned(0, 0, 0)

            def step(i, p, j):
                act.wait_ge(s_clamp, i + 1)
                if not first(i):
                    act.wait_ge(s_v, 3 * i)
                act.activation(U[:], TN[:], ACT.Identity, bias=ngk[:, MID:MID + 1]).then_inc(s_u, 1)
                for n, knot in enumerate(KN):
                    b = n % 2
                    if n >= 2 or not first(i):
                        act.wait_ge(s_cube, NK * i + n - 1)
                    right = knot in RIGHT
                    act.activation(RK[b][:], TN[:], ACT.Relu, bias=(ngk if right else gk)[:, knot:knot + 1],
                                   scale=1.0 if right else -1.0).then_inc(s_r, 1)
                    act.wait_ge(s_r, NK * i + n + 1)
                    act.activation(QK[b][:], RK[b][:], ACT.Square).then_inc(s_q, 1)
                    if n == 3 and not first(i):
                        rows3(i - 1)
                    if n == 8 and not last(i):
                        rows_back(i + 1)
                if not last(i):
                    turned(i + 1, 1 - p, j + p)

            steps(act, NP, step)
            rows3(NP - 1)

        @block.vector
        def _(dve):
            chained = [0]

            def link(ins):
                chained[0] += 1
                ins.then_inc(s_chain, 1)
                dve.wait_ge(s_chain, chained[0])

            dve.wait_ge(s_param, 16 * 10)
            dve.wait_ge(s_ready0, 2)
            link(dve.tensor_scalar(w4[:], w4[:], 0.0, 4.0, ALU.is_ge, ALU.mult))
            w4m = w4[:].rearrange("q (m t) o -> q m (t o)", m=4)
            link(dve.tensor_reduce(wsum[:], w4m.rearrange("q m f -> q f m"), AX_X, ALU.add))
            link(dve.tensor_scalar(wsum[:], wsum[:], 8.0, None, ALU.subtract))
            taps = wsum[:].rearrange("q (a b o) -> q a b o", a=3, b=3)
            for g in range(4):
                rows = slice(g * C, g * C + C)
                for dw in range(3):
                    ins = dve.tensor_copy(WC[rows, :, g + 2 - dw, :], taps[rows, :, dw, :])
                    if (g, dw) == (3, 2):
                        link(ins)
            link(dve.tensor_reduce(BT[:], bias4[:].rearrange("q (m c) -> q c m", m=4), AX_X, ALU.add))
            link(dve.tensor_tensor(gaps[:], gk[:].unsqueeze(2).broadcast_to([128, KNOTS, KNOTS]),
                                   gk[:].unsqueeze(1).broadcast_to([128, KNOTS, KNOTS]), ALU.subtract))
            flat = gaps[:].rearrange("q a b -> q (a b)")

            def gap(a, b):
                lo = KNOTS * a + b
                return flat[:, lo:lo + (KNOTS + 1) * (BASES - 1) + 1:KNOTS + 1]

            for a in range(ORDER + 2):
                others = [b for b in range(ORDER + 2) if b != a]
                link(dve.tensor_tensor(prod[:, a], gap(a, others[0]), gap(a, others[1]), ALU.mult))
                for b in others[2:]:
                    link(dve.tensor_tensor(prod[:, a], prod[:, a], gap(a, b), ALU.mult))
            link(dve.reciprocal(prod[:], prod[:]))
            link(dve.tensor_tensor(wspan[:], gap(ORDER + 1, 0), wsp[:], ALU.mult))
            link(dve.tensor_tensor(prod[:], prod[:], wspan[:].unsqueeze(1).broadcast_to([128, ORDER + 2, BASES]), ALU.mult))
            link(dve.memset(coef[:], 0.0))
            for a in range(ORDER + 2):
                link(dve.tensor_tensor(coef[:, a:a + BASES], coef[:, a:a + BASES], prod[:, a], ALU.add))
            left = MID + 1
            link(dve.tensor_scalar(ngk[:], gk[:], -1.0, None, ALU.mult))
            link(dve.tensor_scalar(shift[:], gk[:, 0:left], gk[:, MID:MID + 1], None, ALU.subtract))
            link(dve.tensor_copy(mom[:, 0], coef[:, 0:left]))
            for n in range(1, ORDER + 1):
                link(dve.tensor_tensor(mom[:, n], mom[:, n - 1], shift[:], ALU.mult))
            link(dve.tensor_reduce(msum[:], mom[:], AX_X, ALU.add))
            for n, factor in enumerate((1.0, -3.0, 3.0, -1.0)):
                ins = dve.tensor_scalar(poly[:, 3 - n:4 - n], msum[:, n:n + 1], factor, None, ALU.mult)
                if n < ORDER:
                    link(ins)
            ins.then_inc(s_set, 1)
            dve.wait_ge(s_set, 1)

            def add_x1(i, p, j):
                dve.wait_ge(s_y, i + 1)
                dve.wait_ge(x_in[p], 16 * (j + 1))
                xg = X[p][:, :].rearrange("q (w o g) -> q g w o", o=8, g=4)
                dve.tensor_tensor(xg, PA[:, :].rearrange("q (g w o) -> q g w o", g=4, o=8), xg,
                                  ALU.add).then_inc(s_x1, 1)

            def normalise(i, p, j):
                for l in range(2, 6):
                    k, before, use = front_use(i, l)
                    dve.wait_ge(free[k], before + 1)
                xi = XT[p][:].rearrange("q w (h d) -> q d w h", d=PAIR)
                for d2 in range(PAIR):
                    for half in range(2):
                        ins = dve.bn_stats(bn1[:, d2, half * 6:half * 6 + 6], xi[:, d2, half * 8:half * 8 + 8])
                ins.then_inc(s_bn1, 1)
                dve.wait_ge(s_bn1, i + 1)
                parts = bn1[:].rearrange("q d (n s) -> q d n s", s=3)
                dve.tensor_reduce(ms1[:], parts[:, :, :, 1], AX_X, ALU.add).then_inc(s_ms1, 1)
                dve.wait_ge(s_pm1, i + 1)
                dve.tensor_copy(mean1[:], pm1).then_inc(s_mean1, 1)
                dve.wait_ge(s_mean1, i + 1)
                dve.tensor_tensor(dv1[:], parts[:, :, :, 1], mean1[:].unsqueeze(2).broadcast_to([128, PAIR, 4]),
                                  ALU.subtract).then_inc(s_dv1, 1)
                dve.wait_ge(s_dv1, i + 1)
                dve.scalar_tensor_tensor(dd1[:], dv1[:], float(H * W // 16), dv1[:], ALU.mult,
                                         ALU.mult).then_inc(s_dd1, 1)
                dve.wait_ge(s_dd1, i + 1)
                dve.tensor_tensor(sv1[:], dd1[:], parts[:, :, :, 2], ALU.add).then_inc(s_sv1, 1)

            def variance1(i):
                dve.wait_ge(s_pv1, i + 1)
                dve.tensor_reduce(vr1[:], pv1.rearrange("q (d n) -> q d n", d=PAIR), AX_X, ALU.add).then_inc(s_vr1, 1)
                dve.wait_ge(s_vr1, i + 1)
                dve.tensor_scalar(ve1[:], vr1[:], EPS, None, ALU.add).then_inc(s_ve1, 1)

            def scale_in(i, p, j):
                dve.wait_ge(s_rs1, i + 1)
                if not first(i):
                    dve.wait_ge(s_r, NK * i)
                xi = XT[p][:].rearrange("q w (h d) -> q d w h", d=PAIR)
                ti = TN[:].rearrange("q (w h d) -> q d w h", h=H, d=PAIR)
                for d2 in range(PAIR):
                    dve.tensor_scalar(ti[:, d2], xi[:, d2], mean1[:, d2:d2 + 1], rstd1[:, d2:d2 + 1],
                                      ALU.subtract, ALU.mult).then_inc(s_tn, 1)
                dve.wait_ge(s_tn, 2 * i + 2)
                dve.tensor_scalar(TN[:], TN[:], gk[:, 0:1], gk[:, KNOTS - 1:KNOTS], ALU.max, ALU.min).then_inc(s_clamp, 1)

            def spectra(i, p, j):
                if later(i):
                    dve.wait_ge(z_out[p], 64 * j)
                dve.wait_ge(st.s_rstd, i + 1)
                for l in range(2):
                    k, before, use = back_use(i, 4 + l)
                    dve.wait_ge(ring, use)
                    dve.tensor_tensor(Z[p][:, l * 8:l * 8 + 8].rearrange("q g (d h) -> q g d h", d=PAIR),
                                      PB[k][:, :].rearrange("q (g d h) -> q g d h", g=8, d=PAIR),
                                      st.rstd[p][:, :, l * 8:l * 8 + 8].rearrange("q d g -> q g d").unsqueeze(3)
                                      .broadcast_to([128, 8, PAIR, M3]), ALU.mult).then_inc(free[k], 1)

            def spline(i, p, j):
                dve.wait_ge(s_u, i + 1)
                dve.tensor_scalar(ACC[:], U[:], poly[:, 3:4], poly[:, 2:3], ALU.mult, ALU.add).then_inc(s_v, 1)
                dve.wait_ge(s_v, 3 * i + 1)
                dve.tensor_tensor(ACC[:], ACC[:], U[:], ALU.mult).then_inc(s_v, 1)
                dve.wait_ge(s_v, 3 * i + 2)
                dve.scalar_tensor_tensor(ACC[:], ACC[:], poly[:, 1:2], U[:], ALU.add, ALU.mult).then_inc(s_v, 1)
                dve.wait_ge(s_v, 3 * i + 3)

                def cube(n):
                    b, knot = n % 2, KN[n]
                    dve.wait_ge(s_q, NK * i + n + 1)
                    if n >= 2:
                        dve.wait_ge(s_acc, NK * i + n - 1)
                    dve.scalar_tensor_tensor(CK[b][:], QK[b][:], coef[:, knot:knot + 1], RK[b][:], ALU.mult,
                                             ALU.mult).then_inc(s_cube, 1)

                def gather(n):
                    dve.wait_ge(s_cube, NK * i + n + 1)
                    if n == 0:
                        ins = dve.scalar_tensor_tensor(ACC[:], ACC[:], poly[:, 0:1], CK[0][:], ALU.add, ALU.add)
                    else:
                        dve.wait_ge(s_acc, NK * i + n)
                        ins = dve.tensor_tensor(ACC[:], ACC[:], CK[n % 2][:], ALU.add)
                    ins.then_inc(s_acc, 1)

                cube(0)
                for n in range(1, NK):
                    cube(n)
                    gather(n - 1)
                    if n == 6 and not first(i):
                        spectra(i - 1, 1 - p, j - 1 + p if not isinstance(j, int) else (i - 1) // 2)
                gather(NK - 1)

            def add_spline(i, p, j):
                dve.wait_ge(s_acc, NK * i + NK)
                xi = XT[p][:].rearrange("q w (h d) -> q d w h", d=PAIR)
                ai = ACC[:].rearrange("q (w h d) -> q d w h", h=H, d=PAIR)
                for d2 in range(PAIR):
                    ins = dve.scalar_tensor_tensor(xi[:, d2], xi[:, d2], 1.0, ai[:, d2], ALU.mult, ALU.add,
                                                   accum_out=sum2[:, d2:d2 + 1])
                    ins.then_inc(s_x2, 1)

            def signs(i, p, j):
                dve.wait_ge(s_pm2, i + 1)
                dve.tensor_copy(mean2[:], pm2).then_inc(s_mean2, 1)
                dve.wait_ge(s_mean2, i + 1)
                if not first(i):
                    dve.wait_ge(s_cv, 4 * i)
                for d2 in range(PAIR):
                    dve.tensor_scalar(SG[:, :, PAIR + d2:PAIR + PAIR * H + d2:PAIR], XT[p][:, :, d2::PAIR],
                                      mean2[:, d2:d2 + 1], 0.5, ALU.is_ge, ALU.subtract).then_inc(s_sg, 1)

            def after_conv(i, p, j, banks):
                if later(i) and banks[0] == 0:
                    dve.wait_ge(x3_out[p], 16 * j)
                    dve.wait_ge(st.s_xn, i - 1)
                for b in banks:
                    dve.wait_ge(s_cv, 4 * i + b + 1)
                    cols = slice(b * 512, b * 512 + 512)
                    dve.tensor_tensor(X3[p][:, cols].rearrange("q (w c) -> q w c", c=C),
                                      PA[:, cols].rearrange("q (w c) -> q w c", c=C),
                                      BT[:].unsqueeze(1).broadcast_to([128, 16, C]), ALU.add).then_inc(s_x3, 1)

            add_x1(0, 0, 0)
            normalise(0, 0, 0)
            variance1(0)
            scale_in(0, 0, 0)

            def step(i, p, j):
                spline(i, p, j)
                add_spline(i, p, j)
                if not last(i):
                    add_x1(i + 1, 1 - p, j + p)
                signs(i, p, j)
                if not last(i):
                    normalise(i + 1, 1 - p, j + p)
                after_conv(i, p, j, (0, 1))
                if not last(i):
                    variance1(i + 1)
                after_conv(i, p, j, (2, 3))
                if not last(i):
                    scale_in(i + 1, 1 - p, j + p)
                dve.wait_ge(s_x3, 4 * i + 4)
                row_stats_start(dve, st, i, X3[p][:, :])
                row_stats_middle(dve, st, i)
                row_stats_end(dve, st, i, p)

            steps(dve, NP, step, peel=4)
            spectra(NP - 1, 1, NP // 2 - 1)

        @block.tensor
        def _(pe):
            pe.wait_ge(s_const, 16 * 9)
            pe.wait_ge(s_set, 1)

            def back0(i, p, j):
                pe.wait_ge(im_in[p], 32 * (j + 1))
                for l in range(2):
                    k, before, use = front_use(i, l)
                    if not (isinstance(before, int) and before == 0):
                        pe.wait_ge(free[k], before)
                    bank = PB[k][:, :].rearrange("q (g r h d) -> q g d r h", g=2, r=2, d=PAIR)
                    for g in range(2):
                        for d2 in range(PAIR):
                            ins = pe.matmul(bank[:, g, d2], IM[p][:, d2, 2 * l + g::4], gh[:, :],
                                            start=True, stop=True)
                    ins.then_inc(ring, 1)
                for l in range(2):
                    k, before, use = front_use(i, l)
                    pe.wait_ge(free[k], before + 1)
                if later(i):
                    pe.wait_ge(s_x3, 4 * (i - 1))
                for g in range(4):
                    for ri in range(2):
                        ins = pe.matmul(PA[:, g * 512:g * 512 + 512], AI[:, g, ri], gw[:, ri],
                                        start=(ri == 0), stop=(ri == 1))
                ins.then_inc(s_y, 1)

            def turn(i, p, j):
                pe.wait_ge(s_x1, i + 1)
                for l in range(2, 6):
                    k, before, use = front_use(i, l)
                    if not (isinstance(before, int) and before == 0):
                        pe.wait_ge(free[k], before)
                    for n in range(4):
                        at = (4 * (l - 2) + n) * 128
                        ins = pe.transpose(PB[k][:, n * 128:n * 128 + 128], X[p][:, at:at + 128], ident[:, :])
                    ins.then_inc(ring, 1)

            def mean1_tensor(i):
                pe.wait_ge(s_ms1, i + 1)
                pe.matmul(pm1, gavg[:, :], ms1[:], start=True, stop=True).then_inc(s_pm1, 1)

            def variance1_tensor(i):
                pe.wait_ge(s_sv1, i + 1)
                pe.matmul(pv1, gsum[:, :], sv1[:].rearrange("q d n -> q (d n)"), start=True, stop=True).then_inc(s_pv1, 1)

            def conv(i, p, j, banks):
                if banks[0] == 0:
                    pe.wait_ge(s_sg, 2 * i + 2)
                    pe.wait_ge(s_x1, i + 2 if not last(i) else i + 1)
                for b in banks:
                    lo = b * 512
                    for n in range(4):
                        pe.matmul(PA[:, lo + n * 128:lo + n * 128 + 128], XT[p][:, 4 * b + n], ident[:, :],
                                  start=(n == 0), stop=False, skip_group_check=True)
                    for blk in range(max(4 * b - 1, 0), min(4 * b + 5, 16)):
                        c0 = max((4 * blk - 1) * C, lo)
                        c1 = min((4 * blk + 5) * C, lo + 512)
                        off = (4 * blk - 1) * C
                        for dh in range(3):
                            ins = pe.matmul(PA[:, c0:c1], SG[:, blk, PAIR * dh:PAIR * dh + 128],
                                            WC[:, dh].rearrange("q w c -> q (w c)")[:, c0 - off:c1 - off],
                                            start=False, stop=(blk == min(4 * b + 4, 15) and dh == 2),
                                            skip_group_check=True)
                    ins.then_inc(s_cv, 1)

            def forward3(i, p, j):
                pe.wait_ge(st.s_xn, i + 1)
                for l in range(4):
                    k, before, use = back_use(i, l)
                    pe.wait_ge(free[k], before)
                    for n in range(4):
                        at = (4 * l + n) * 128
                        ins = pe.matmul(PB[k][:, n * 128:n * 128 + 128], XN3[:, at:at + 128], fh[:, :],
                                        start=True, stop=True)
                    ins.then_inc(ring, 1)
                for l in range(2):
                    k, before, use = back_use(i, 4 + l)
                    pe.wait_ge(free[k], before)
                    for m in range(2):
                        kk, bb, uu = back_use(i, 2 * l + m)
                        pe.wait_ge(free[kk], bb + 1)
                    hv = hw[:].rearrange("q (g r n) -> q r g n", g=G, r=2)
                    for ri in range(2):
                        ins = pe.matmul(PB[k][:, :], fw[:, ri], hv[:, ri, l * 8:l * 8 + 8],
                                        start=(ri == 0), stop=(ri == 1))
                    ins.then_inc(ring, 1)

            back0(0, 0, 0)
            turn(0, 0, 0)
            mean1_tensor(0)
            variance1_tensor(0)

            def step(i, p, j):
                if not first(i):
                    forward3(i - 1, 1 - p, j)
                if not last(i):
                    back0(i + 1, 1 - p, j + p)
                pe.wait_ge(s_x2, 2 * i + 2)
                pe.matmul(pm2, gsum[:, :], sum2[:], start=True, stop=True).then_inc(s_pm2, 1)
                if not last(i):
                    turn(i + 1, 1 - p, j + p)
                if last(i):
                    conv(i, p, j, (0, 1, 2, 3))
                else:
                    conv(i, p, j, (0,))
                    mean1_tensor(i + 1)
                    conv(i, p, j, (1,))
                    variance1_tensor(i + 1)
                    conv(i, p, j, (2, 3))
                row_mean_tensor(pe, st, i)
                row_variance_tensor(pe, st, i)

            steps(pe, NP, step)
            forward3(NP - 1, 1, 0)


def phase_modes3(nc, consts, conv_w, spectra3_dram, mixed_dram):
    with ExitStack() as ctx:
        pl = Places(nc, ctx, "D")
        XD = [pl.sb(f"x{p}", [128, 2 * D, M3]) for p in range(2)]
        WB = [pl.sb(f"w{p}", [128, M3, 4, C]) for p in range(2)]
        GS = [pl.sb(f"g{p}", [128, M3, 128]) for p in range(2)]
        P = [pl.ps(f"p{b}") for b in range(8)]
        s_zero = pl.sem("zero")
        x_in = [pl.sem(f"x_in{p}") for p in range(2)]
        w_in = [pl.sem(f"w_in{p}") for p in range(2)]
        g_out = [pl.sem(f"g_out{p}") for p in range(2)]
        s_mm = pl.sem("mm")
        s_g = [pl.sem(f"g{e}") for e in range(2)]
        TURNS = M3 // 4
        xv = spectra3_dram.rearrange("(t k) g c r f -> t (k g c) r f", k=4)
        wv = conv_w.rearrange("h (t k) c o -> t k c h o", k=4)
        block = ctx.enter_context(nc.Block())

        def copy_out(eng, copy, share):
            def step(i, p, j):
                if later(i):
                    eng.wait_ge(g_out[p], 16 * j)
                for b in range(share, 8, 2):
                    eng.wait_ge(s_mm, 8 * i + b + 1)
                    copy(GS[p][:, 4 * b:4 * b + 4].rearrange("q h n -> q (h n)"), P[b][:, :]).then_inc(s_g[share], 1)

            steps(eng, TURNS, step)

        @block.sync
        def _(sp):
            sp.wait_ge(s_zero, 2)

            def load(i, p, j):
                if later(i):
                    sp.wait_ge(s_mm, 8 * (i - 1))
                sp.dma_start(XD[p][:].rearrange("q (r d) h -> q r (d h)", r=2), xv[i]).then_inc(x_in[p], 16)
                for k in range(4):
                    sp.dma_start(WB[p][k * C:k * C + C, :, k, :], wv[i, k]).then_inc(w_in[p], 16)

            steps(sp, TURNS, load)

        @block.gpsimd
        def _(pool):
            for p in range(2):
                pool.memset(WB[p][:], 0.0).then_inc(s_zero, 1)
            dst = mixed_dram.rearrange("r d h (t n) -> t (r d) h n", n=128)

            def store(i, p, j):
                for e in range(2):
                    pool.wait_ge(s_g[e], 4 * i + 4)
                pool.dma_start(dst[i], GS[p][:]).then_inc(g_out[p], 16)

            steps(pool, TURNS, store)
            for p in range(2):
                pool.wait_ge(g_out[p], 16 * (TURNS // 2))

        @block.vector
        def _(dve):
            copy_out(dve, lambda d, s: dve.tensor_copy(d, s), 0)

        @block.scalar
        def _(act):
            copy_out(act, lambda d, s: act.activation(d, s, ACT.Copy), 1)

        @block.tensor
        def _(pe):
            def step(i, p, j):
                pe.wait_ge(x_in[p], 16 * (j + 1))
                pe.wait_ge(w_in[p], 64 * (j + 1))
                for h in range(M3):
                    b = h // 4
                    if h % 4 == 0 and not (isinstance(i, int) and i == 0):
                        pe.wait_ge(s_g[b % 2], 4 * (i - 1) + b // 2 + 1)
                    ins = pe.matmul(P[b][:, h % 4 * 128:h % 4 * 128 + 128], XD[p][:, :, h],
                                    WB[p][:, h].rearrange("q k o -> q (k o)"), start=True, stop=True)
                    if h % 4 == 3:
                        ins.then_inc(s_mm, 1)

            steps(pe, TURNS, step)


def phase_back3(nc, consts, mixed_dram, x3_dram, out):
    with ExitStack() as ctx:
        pl = Places(nc, ctx, "E")
        X = [pl.sb(f"x{p}", [128, ROW]) for p in range(2)]
        IM = [pl.sb(f"im{p}", [64, PAIR, M3 * C]) for p in range(2)]
        AI = [pl.sb(f"ai{p}", [128, 8, 2, 128]) for p in range(2)]
        gh = pl.sb("gh", [64, 128])
        gw = pl.sb("gw", [128, 2, 256])
        PR = [pl.ps(f"pr{b}") for b in range(4)]
        PY = [pl.ps(f"py{b}") for b in range(4)]
        s_const = pl.sem("const")
        x_in = [pl.sem(f"x_in{p}") for p in range(2)]
        im_in = [pl.sem(f"im_in{p}") for p in range(2)]
        o_out = [pl.sem(f"o_out{p}") for p in range(2)]
        s_r = pl.sem("r")
        s_ai = pl.sem("ai")
        s_y = pl.sem("y")
        s_o = pl.sem("o")
        xv = x3_dram.rearrange("(n d) h f -> n h d f", d=PAIR)
        ov = out.rearrange("(n d) h w c -> n h d (w c)", d=PAIR)
        block = ctx.enter_context(nc.Block())

        @block.sync
        def _(sp):
            sp.dma_start(gh[:], consts["gh3"]).then_inc(s_const, 16)
            sp.dma_start(gw[:], consts["gw3"]).then_inc(s_const, 16)

            def load(i, p, j):
                if later(i):
                    sp.wait_ge(s_r, 4 * (i - 1))
                for ri in range(2):
                    sp.dma_start(IM[p][ri * 32:ri * 32 + 32],
                                 mixed_dram[ri, bass.ds(i * PAIR, PAIR)].rearrange("d k f -> k d f")).then_inc(im_in[p], 16)
                if later(i):
                    sp.wait_ge(o_out[p], 16 * j)
                sp.dma_start(X[p][:, :], xv[i]).then_inc(x_in[p], 16)

            steps(sp, NP, load)

        @block.scalar
        def _(act):
            def step(i, p, j):
                for b in range(4):
                    act.wait_ge(s_r, 4 * i + b + 1)
                    if b == 0 and later(i):
                        act.wait_ge(s_y, 4 * (i - 1))
                    act.activation(AI[p][:, 2 * b:2 * b + 2].rearrange("q g r n -> q (g r n)"), PR[b][:, :],
                                   ACT.Copy).then_inc(s_ai, 1)

            steps(act, NP, step)

        @block.gpsimd
        def _(pool):
            def store(i, p, j):
                pool.wait_ge(s_o, 4 * i + 4)
                pool.dma_start(ov[i], X[p][:, :]).then_inc(o_out[p], 16)

            steps(pool, NP, store)
            for p in range(2):
                pool.wait_ge(o_out[p], 16 * (NP // 2))

        @block.vector
        def _(dve):
            def step(i, p, j):
                dve.wait_ge(x_in[p], 16 * (j + 1))
                xg = X[p][:, :].rearrange("q (w o g) -> q g w o", o=4, g=8)
                for b in range(4):
                    dve.wait_ge(s_y, 4 * i + b + 1)
                    dve.tensor_tensor(xg[:, 2 * b:2 * b + 2], PY[b][:, :].rearrange("q (g w o) -> q g w o", g=2, o=4),
                                      xg[:, 2 * b:2 * b + 2], ALU.add).then_inc(s_o, 1)

            steps(dve, NP, step)

        @block.tensor
        def _(pe):
            pe.wait_ge(s_const, 32)

            def rows(i, p, j):
                pe.wait_ge(im_in[p], 32 * (j + 1))
                for b in range(4):
                    if not (isinstance(i, int) and i == 0):
                        pe.wait_ge(s_ai, 4 * (i - 1) + b + 1)
                    bank = PR[b][:, :].rearrange("q (g r h d) -> q g d r h", g=2, r=2, d=PAIR)
                    for g in range(2):
                        for d2 in range(PAIR):
                            ins = pe.matmul(bank[:, g, d2], IM[p][:, d2, 2 * b + g::8], gh[:, :],
                                            start=True, stop=True)
                    ins.then_inc(s_r, 1)

            def cols(i, p, j):
                for b in range(4):
                    pe.wait_ge(s_ai, 4 * i + b + 1)
                    if not (isinstance(i, int) and i == 0):
                        pe.wait_ge(s_o, 4 * (i - 1) + b + 1)
                    for g in range(2):
                        for ri in range(2):
                            ins = pe.matmul(PY[b][:, g * 256:g * 256 + 256], AI[p][:, 2 * b + g, ri], gw[:, ri],
                                            start=(ri == 0), stop=(ri == 1))
                    ins.then_inc(s_y, 1)

            def step(i, p, j):
                if not (isinstance(i, int) and i == NP - 1):
                    rows(i + 1, 1 - p, j + p)
                cols(i, p, j)

            rows(0, 0, 0)
            steps(pe, NP, step)


def tables():
    import numpy as np

    kd = np.r_[0:M, -M:0]
    n = np.arange(D)
    full = 2 * D - 1
    two, sc = np.eye(2), 1.0 / full ** 1.5

    def cis(k, n, period):
        a = 2 * np.pi * np.outer(k, n) / period
        return np.cos(a), np.sin(a)

    def forward_rows(cos, sin, scale=1.0):
        return scale * np.einsum("de,rkh->hdrek", two, np.stack([cos, -sin])).reshape(128, -1)

    def inverse_rows(cos, sin):
        return np.block([[cos, sin], [-sin, cos]])

    c, s = cis(kd, n, full)
    out = {"fh0": forward_rows(c, s, sc), "gh0": inverse_rows(c, s), "ed0": inverse_rows(c, s)}
    fre = np.concatenate([c.T, s.T])
    fim = np.concatenate([-s.T, c.T])
    roles = np.stack([np.stack([fre, fim], -1), np.stack([-fim, fre], -1)], 1)
    roles = roles.reshape(128, 2, 2, 2, 8, 2).transpose(0, 1, 3, 2, 4, 5)
    out["fd0"] = roles.reshape(128, 128)
    cw, sw = cis(np.arange(KW), n, full)
    out["fw0"] = np.stack([
        np.einsum("ce,rkw->cwrek", two, np.stack([cw, -sw])).reshape(128, 64),
        np.einsum("ce,rkw->cwrek", two, np.stack([sw, cw])).reshape(128, 64)], 1)
    weight = np.where(np.arange(KW) == 0, 1.0, 2.0)[:, None] * sc
    out["gw0"] = np.stack([np.einsum("kw,oq->kowq", weight * t, np.eye(8)).reshape(128, 512)
                           for t in (cw, -sw)], 1)
    k3 = np.arange(M3)
    c3, s3 = cis(k3, n, H)
    out["fh3"] = forward_rows(c3, s3)
    out["gh3"] = inverse_rows(c3, s3)
    out["fw3"] = np.stack([
        np.einsum("ce,rkw->cwerk", two, np.stack([c3, -s3])).reshape(128, 128),
        np.einsum("ce,rkw->cwerk", two, np.stack([s3, c3])).reshape(128, 128)], 1)
    weight = np.where(k3 == 0, 1.0, 2.0)[:, None] / (H * W)
    out["gw3"] = np.stack([np.einsum("kw,oq->kowq", weight * t, np.eye(4)).reshape(128, 256)
                           for t in (c3, -s3)], 1)
    image = np.kron(np.ones((64, 64)), np.eye(2))
    out["avg"] = image / 128
    out["var"] = np.stack([np.repeat((np.arange(128) % 2 == d)[:, None], 128, 1) / (H * W * 2.0)
                           for d in range(2)], 1)
    group = (np.arange(128) % 32) // 2
    same = (group[:, None] == group[None, :]).astype(float)
    out["gavg"] = same / 32
    out["gsum"] = same / (H * W * 2.0)
    out["ident"] = np.eye(128)
    out["diag8"] = (np.arange(128)[:, None] % 8 == np.arange(8)[None, :]).astype(float)
    return {k: np.ascontiguousarray(v, dtype=np.float32) for k, v in out.items()}


def build(nc, args, consts, out):

    def scratch(name, shape):
        return nc.dram_tensor(name, shape, F32).ap()

    spectra = scratch("spectra", [2, D, 2, 32, 256])
    modes = scratch("modes", [32, 128, 256])
    images = scratch("images", [2, D, KH, KW * C])
    x3 = scratch("x3", [D, H, ROW])
    spectra3 = scratch("spectra3", [M3, G, 2, 2, D * M3])
    mixed = scratch("mixed", [2, D, M3, M3 * C])
    weights = [(args[f"L0_conv_w{n}r"], args[f"L0_conv_w{n}i"]) for n in range(1, 5)]
    params = (args["L1_conv_grid"], args["L1_conv_W"], args["L2_conv_W"], args["L2_conv_b"])
    phase_forward(nc, args["x"], consts, spectra)
    phase_depth(nc, consts, spectra, weights, modes, images)
    phase_images(nc, args["x"], consts, params, images, x3, spectra3)
    phase_modes3(nc, consts, args["L3_conv_W"], spectra3, mixed)
    phase_back3(nc, consts, mixed, x3, out)


_INS = ["x"] + [f"L0_conv_w{n}{part}" for n in range(1, 5) for part in "ri"] + [
    "L1_conv_grid", "L1_conv_W", "L2_conv_W", "L2_conv_b", "L3_conv_W"]


def kernel(**inputs):
    import numpy as np
    import concourse.bacc as bacc
    from concourse.bass_utils import run_bass_kernel_spmd

    nc = bacc.Bacc("TRN2", target_bir_lowering=False, num_devices=1)
    arrays, args, consts = {}, {}, {}
    for name in _INS:
        arrays[f"in_{name}"] = np.ascontiguousarray(inputs[name])
        args[name] = nc.dram_tensor(f"in_{name}", arrays[f"in_{name}"].shape, F32, kind="ExternalInput").ap()
    for name, table in tables().items():
        arrays[f"table_{name}"] = table
        consts[name] = nc.dram_tensor(f"table_{name}", table.shape, F32, kind="ExternalInput").ap()
    out = nc.dram_tensor("out_y", (D, H, W, C), F32, kind="ExternalOutput").ap()
    build(nc, args, consts, out)
    r = run_bass_kernel_spmd(nc, [arrays], core_ids=[0])
    return r.results[0]["out_y"]
```

```python
from contextlib import ExitStack

import concourse.bass as bass
from concourse import mybir

F32 = mybir.dt.float32
BF16 = mybir.dt.bfloat16
ALU = mybir.AluOpType
ACT = mybir.ActivationFunctionType
AX_X = mybir.AxisListType.X

D = H = W = 64
C = 32
G = 16
PAIR = 2
NP = D // PAIR
M = 16
KH = 2 * M
KW = M
M3 = 32
KNOTS, BASES, ORDER = 12, 8, 3
MID = 5
EPS = 1e-5
ROW = W * C


def later(i):
    return not isinstance(i, int) or i >= 2


def steps(eng, n, body, peel=2):
    for i in range(peel):
        body(i, i % 2, i // 2)
    with eng.Fori(peel // 2, n // 2 - 1) as j:
        body(2 * j, 0, j)
        body(2 * j + 1, 1, j)
    body(n - 2, 0, n // 2 - 1)
    body(n - 1, 1, n // 2 - 1)


class Places:

    def __init__(self, nc, ctx, tag):
        self.nc, self.ctx, self.tag = nc, ctx, tag

    def sb(self, name, shape, dt=F32):
        return self.ctx.enter_context(self.nc.sbuf_tensor(f"{self.tag}_{name}", shape, dt))

    def ps(self, name, cols=512):
        return self.ctx.enter_context(self.nc.psum_tensor(f"{self.tag}_{name}", [128, cols], F32))

    def sem(self, name):
        return self.ctx.enter_context(self.nc.semaphore(f"{self.tag}_{name}"))


class RowStats:

    def __init__(self, pl, psum):
        self.bn = pl.sb("bn", [128, G, 6])
        self.ms = pl.sb("ms", [128, G])
        self.mu = pl.sb("mu", [128, G])
        self.dev = pl.sb("dev", [128, G, 2])
        self.dev2 = pl.sb("dev2", [128, G, 2])
        self.sq = pl.sb("sq", [128, G, 2])
        self.vr = pl.sb("vr", [128, PAIR, G])
        self.ve = [pl.sb(f"ve{p}", [128, PAIR, G]) for p in range(2)]
        self.rstd = [pl.sb(f"rstd{p}", [128, PAIR, G]) for p in range(2)]
        self.mhalf = pl.sb("mhalf", [128, PAIR, G])
        self.avg = pl.sb("avg", [128, 128])
        self.var = pl.sb("var", [128, PAIR, 128])
        self.pm = psum[:, 0:G]
        self.pv = psum[:, 64:64 + PAIR * G * 2]
        self.s_bn = pl.sem("s_bn")
        self.s_ms = pl.sem("s_ms")
        self.s_pm = pl.sem("s_pm")
        self.s_mu = pl.sem("s_mu")
        self.s_dev = pl.sem("s_dev")
        self.s_dev2 = pl.sem("s_dev2")
        self.s_sq = pl.sem("s_sq")
        self.s_pv = pl.sem("s_pv")
        self.s_vr = pl.sem("s_vr")
        self.s_ve = pl.sem("s_ve")
        self.s_rstd = pl.sem("s_rstd")
        self.s_xn = pl.sem("s_xn")
        self.s_mh = pl.sem("s_mh")


def center(eng, st, mean, x, out):
    eng.tensor_tensor(out.rearrange("p (g c w) -> p g c w", g=G, c=2),
                      x.rearrange("p (w g c) -> p g c w", g=G, c=2),
                      mean.unsqueeze(2).unsqueeze(3).broadcast_to([128, G, 2, W]),
                      ALU.subtract).then_inc(st.s_xn, 1)


def row_stats_start(dve, st, i, x):
    xg = x.rearrange("p (w g c) -> p g w c", g=G, c=2)
    for g in range(G):
        ins = dve.bn_stats(st.bn[:, g, :], xg[:, g])
    ins.then_inc(st.s_bn, 1)
    dve.wait_ge(st.s_bn, i + 1)
    dve.tensor_tensor(st.ms[:, :], st.bn[:, :, 1], st.bn[:, :, 4], ALU.add).then_inc(st.s_ms, 1)


def row_stats_middle(dve, st, i):
    dve.wait_ge(st.s_pm, i + 1)
    if not (isinstance(i, int) and i == 0):
        dve.wait_ge(st.s_xn, i)
    dve.tensor_copy(st.mu[:, :], st.pm).then_inc(st.s_mu, 1)
    dve.tensor_tensor(st.dev[:, :, :], st.bn[:, :, 1::3], st.pm.unsqueeze(2).broadcast_to([128, G, 2]),
                      ALU.subtract).then_inc(st.s_dev, 1)
    dve.wait_ge(st.s_dev, i + 1)
    dve.scalar_tensor_tensor(st.dev2[:, :, :], st.dev[:, :, :], float(W), st.dev[:, :, :],
                             ALU.mult, ALU.mult).then_inc(st.s_dev2, 1)
    dve.wait_ge(st.s_dev2, i + 1)
    dve.tensor_tensor(st.sq[:, :, :], st.dev2[:, :, :], st.bn[:, :, 2::3], ALU.add).then_inc(st.s_sq, 1)


def row_stats_end(dve, st, i, p):
    dve.wait_ge(st.s_pv, i + 1)
    dve.tensor_reduce(st.vr[:, :, :], st.pv.rearrange("p (d g c) -> p d g c", d=PAIR, c=2), AX_X,
                      ALU.add).then_inc(st.s_vr, 1)
    if later(i):
        dve.wait_ge(st.s_rstd, i - 1)
    dve.wait_ge(st.s_vr, i + 1)
    dve.tensor_scalar(st.ve[p][:, :, :], st.vr[:, :, :], EPS, None, ALU.add).then_inc(st.s_ve, 1)


def row_mean_tensor(pe, st, i):
    pe.wait_ge(st.s_ms, i + 1)
    pe.matmul(st.pm, st.avg[:, :], st.ms[:, :], start=True, stop=True).then_inc(st.s_pm, 1)


def row_variance_tensor(pe, st, i):
    pe.wait_ge(st.s_sq, i + 1)
    for d2 in range(PAIR):
        ins = pe.matmul(st.pv[:, d2 * 32:d2 * 32 + 32], st.var[:, d2, :],
                        st.sq[:, :, :].rearrange("p g c -> p (g c)"), start=True, stop=True)
    ins.then_inc(st.s_pv, 1)


def row_stats_root(pool, st, i, p):
    pool.wait_ge(st.s_ve, i + 1)
    pool.tensor_tensor(st.rstd[p][:, :, :], st.ve[p][:, :, :], st.mhalf[:, :, :], ALU.pow).then_inc(st.s_rstd, 1)


def phase_forward(nc, x, consts, spectra_dram):
    with ExitStack() as ctx:
        pl = Places(nc, ctx, "A")
        X = [pl.sb(f"x{p}", [128, ROW]) for p in range(2)]
        XN = [pl.sb(f"xn{p}", [128, ROW]) for p in range(2)]
        hw = [pl.sb(f"rows{p}", [128, 4 * 512]) for p in range(2)]
        Z = [pl.sb(f"z{p}", [128, PAIR, KH, 8]) for p in range(2)]
        fh = pl.sb("fh", [128, 128])
        fw = pl.sb("fw", [128, 2, 64])
        P_h = [pl.ps(f"ph{b}") for b in range(4)]
        P_z = [pl.ps(f"pz{b}") for b in range(2)]
        P_s = pl.ps("pstat")
        st = RowStats(pl, P_s)
        s_const = pl.sem("const")
        x_in = [pl.sem(f"x_in{p}") for p in range(2)]
        z_out = [pl.sem(f"z_out{p}") for p in range(2)]
        s_h = pl.sem("h")
        s_rows = pl.sem("rows")
        s_w = pl.sem("w")
        s_z = pl.sem("z")
        xv = x.rearrange("(n d) h w c -> n h d (w c)", d=PAIR)
        block = ctx.enter_context(nc.Block())

        @block.sync
        def _(sp):
            for dst, name in ((fh, "fh0"), (fw, "fw0"), (st.avg, "avg"), (st.var, "var")):
                sp.dma_start(dst[:], consts[name]).then_inc(s_const, 16)

            def load(i, p, j):
                if later(i):
                    sp.wait_ge(st.s_xn, i - 1)
                sp.dma_start(X[p][:, :], xv[i]).then_inc(x_in[p], 16)

            steps(sp, NP, load)

        @block.scalar
        def _(act):
            def step(i, p, j):
                for b in range(4):
                    act.wait_ge(s_h, 4 * i + b + 1)
                    if b == 0 and later(i):
                        act.wait_ge(s_w, i - 1)
                    act.activation(hw[p][:, b * 512:(b + 1) * 512], P_h[b][:, :], ACT.Copy).then_inc(s_rows, 1)
                act.wait_ge(s_z, 2 * i + 2)
                for half in range(2):
                    for ri in range(2):
                        lo = half * 64 + ri * 32
                        act.dma_start(spectra_dram[ri, bass.ds(i * PAIR, PAIR), half].rearrange("d k f -> k d f"),
                                      Z[p][lo:lo + 32].rearrange("k d h g -> k d (h g)")).then_inc(z_out[p], 16)

            steps(act, NP, step)
            for p in range(2):
                act.wait_ge(z_out[p], 64 * (NP // 2))

        @block.gpsimd
        def _(pool):
            pool.memset(st.mhalf[:, :, :], -0.5).then_inc(st.s_mh, 1)
            pool.wait_ge(st.s_mh, 1)

            def root(i, p, j):
                if later(i):
                    pool.wait_ge(s_z, 2 * (i - 1))
                row_stats_root(pool, st, i, p)

            steps(pool, NP, root)

        @block.vector
        def _(dve):
            def stats(i, p, j):
                dve.wait_ge(x_in[p], 16 * (j + 1))
                row_stats_start(dve, st, i, X[p][:, :])
                row_stats_middle(dve, st, i)
                if later(i):
                    dve.wait_ge(s_h, 4 * (i - 1))
                dve.wait_ge(st.s_mu, i + 1)
                center(dve, st, st.mu[:, :], X[p][:, :], XN[p][:, :])
                row_stats_end(dve, st, i, p)

            def step(i, p, j):
                if not (isinstance(i, int) and i == NP - 1):
                    stats(i + 1, 1 - p, j + p)
                dve.wait_ge(s_w, i + 1)
                dve.wait_ge(st.s_rstd, i + 1)
                if later(i):
                    dve.wait_ge(z_out[p], 64 * j)
                for half in range(2):
                    rows = slice(half * 64, half * 64 + 64)
                    ins = dve.tensor_tensor(
                        Z[p][rows].rearrange("p d h g -> p g d h"),
                        P_z[p][rows].rearrange("p (g d h) -> p g d h", g=8, d=PAIR),
                        st.rstd[p][rows, :, half * 8:half * 8 + 8].rearrange("p d g -> p g d").unsqueeze(3)
                        .broadcast_to([64, 8, PAIR, KH]), ALU.mult)
                    ins.then_inc(s_z, 1)

            stats(0, 0, 0)
            steps(dve, NP, step)

        @block.tensor
        def _(pe):
            pe.wait_ge(s_const, 64)

            def step(i, p, j):
                more = not (isinstance(i, int) and i == NP - 1)
                pe.wait_ge(st.s_xn, i + 1)
                for g in range(G):
                    if g % 4 == 0 and not (isinstance(i, int) and i == 0):
                        pe.wait_ge(s_rows, 4 * (i - 1) + g // 4 + 1)
                    ins = pe.matmul(P_h[g // 4][:, g % 4 * 128:g % 4 * 128 + 128], XN[p][:, g * 128:g * 128 + 128], fh[:, :],
                                    start=True, stop=True)
                    if g % 4 == 3:
                        ins.then_inc(s_h, 1)
                if more:
                    row_mean_tensor(pe, st, i + 1)
                pe.wait_ge(s_rows, 4 * i + 4)
                if later(i):
                    pe.wait_ge(s_z, 2 * (i - 1))
                hv = hw[p][:, :].rearrange("p (g r n) -> p r g n", g=G, r=2)
                for ri in range(2):
                    for half in range(2):
                        ins = pe.matmul(P_z[p][half * 64:half * 64 + 64, :], fw[:, ri, :],
                                        hv[:, ri, half * 8:half * 8 + 8], start=(ri == 0), stop=(ri == 1))
                ins.then_inc(s_w, 1)
                if more:
                    row_variance_tensor(pe, st, i + 1)

            row_mean_tensor(pe, st, 0)
            row_variance_tensor(pe, st, 0)
            steps(pe, NP, step)


def phase_depth(nc, consts, spectra_dram, weights, modes_dram, images_dram):
    with ExitStack() as outer:
        S = outer.enter_context(nc.sbuf_tensor("B_modes", [128, 32, 512], F32))
        plo = Places(nc, outer, "B")
        WT = [plo.sb(f"w{p}", [128, C, M * M]) for p in range(2)]
        w_in = [plo.sem(f"w_in{p}") for p in range(2)]

        def load_weights(sp, p, corner, m1):
            hh, dh = divmod(corner, 2)
            for q in range(2):
                for part in range(2):
                    w = weights[dh * 2 + hh][part]
                    lo = q * 64 + part * 32
                    sp.dma_start(WT[p][lo:lo + 32],
                                 w.rearrange("i o a b c -> i a o (b c)")[:, m1 + 8 * q]
                                 if isinstance(m1, int) else
                                 w.rearrange("i o a b c -> i a o (b c)")[:, bass.ds(m1 + 8 * q, 1)]
                                 .rearrange("i x o f -> i (x o) f")).then_inc(w_in[p], 16)

        with ExitStack() as ctx:
            pl = Places(nc, ctx, "B1")
            D1 = pl.sb("d1", [128, 4, KW, 256])
            T = [pl.sb(f"t{p}", [128, KH, C]) for p in range(2)]
            fd = pl.sb("fd", [128, 4, 32])
            P = [[pl.ps(f"p{p}{hh}") for hh in range(2)] for p in range(2)]
            s_in = pl.sem("in")
            s_t = [pl.sem(f"t{c}") for c in range(2)]
            s_f = pl.sem("f")
            s_s = [pl.sem(f"s{hh}") for hh in range(2)]
            block = ctx.enter_context(nc.Block())

            def lay_out(copy, eng, c2, i, p, j):
                if later(i):
                    eng.wait_ge(s_f, 2 * (i - 1))
                src = D1[:].rearrange("q (a c) k (h g) -> q c k a h g", c=2, g=8)[:, c2]
                src = src[:, i if isinstance(i, int) else bass.ds(i, 1)]
                if not isinstance(i, int):
                    src = src.rearrange("q o a h g -> q (o a) h g")
                dst = T[p][:].rearrange("q h (a g c) -> q c a h g", a=2, g=8)[:, c2]
                copy(dst, src).then_inc(s_t[c2], 1)

            def keep(copy, eng, hh, i, p, j):
                eng.wait_ge(s_f, 2 * i + hh + 1)
                dst = S[:, hh * 16:hh * 16 + 16, :].rearrange("q t (m a r b) -> q a b m t r", m=M, a=2, r=2)[:, p]
                dst = dst[:, j if isinstance(j, int) else bass.ds(j, 1)]
                if not isinstance(j, int):
                    dst = dst.rearrange("q o m t r -> q (o m) t r")
                src = P[p][hh][:, :].rearrange("q (m t r) -> q m t r", m=M, r=2)
                copy(dst, src).then_inc(s_s[hh], 1)

            @block.sync
            def _(sp):
                sp.dma_start(fd[:], consts["fd0"].rearrange("p (r f) -> p r f", r=4)).then_inc(s_in, 16)
                src = spectra_dram.rearrange("r d h (c k) f -> (r d) (h c) k f", c=2)
                for a in range(4):
                    sp.dma_start(D1[:, a], src[:, a]).then_inc(s_in, 16)
                for m1 in range(2):
                    load_weights(sp, m1, 0, m1)

            def copier(eng, copy, share):
                eng.wait_ge(s_in, 80)
                lay_out(copy, eng, share, 0, 0, 0)

                def step(i, p, j):
                    if not (isinstance(i, int) and i == KW - 1):
                        lay_out(copy, eng, share, i + 1, 1 - p, j + p)
                    keep(copy, eng, share, i, p, j)

                steps(eng, KW, step)

            @block.scalar
            def _(act):
                copier(act, lambda d, s: act.activation(d, s, ACT.Copy), 0)

            @block.vector
            def _(dve):
                copier(dve, lambda d, s: dve.tensor_copy(d, s), 1)

            @block.tensor
            def _(pe):
                pe.wait_ge(s_in, 80)

                def step(i, p, j):
                    for c2 in range(2):
                        pe.wait_ge(s_t[c2], i + 1)
                    for kh in range(KH):
                        hh, m2 = divmod(kh, M)
                        if m2 == 0 and later(i):
                            pe.wait_ge(s_s[hh], i - 1)
                        for rows in range(4):
                            q, role = divmod(rows, 2)
                            ins = pe.matmul(P[p][hh][rows * 32:rows * 32 + 32, m2 * 32:m2 * 32 + 32],
                                            T[p][:, kh, :], fd[:, role * 2 + q, :], start=True, stop=True)
                        if m2 == M - 1:
                            ins.then_inc(s_f, 1)

                steps(pe, KW, step)

        with ExitStack() as ctx:
            pl = Places(nc, ctx, "B2")
            SZ = [pl.sb(f"sz{p}", [128, 32, 32]) for p in range(2)]
            cross = pl.sb("cross", [128, 64 * C])
            R = [pl.sb(f"r{p}", [128, 8 * C]) for p in range(2)]
            diag = pl.sb("diag", [128, 8])
            P = [pl.ps(f"p{p}", 4 * 512) for p in range(2)]
            s_const = pl.sem("const")
            s_zero = pl.sem("zero")
            r_out = [pl.sem(f"r_out{p}") for p in range(2)]
            s_sz = pl.sem("sz")
            s_mm = pl.sem("mm")
            s_cross = pl.sem("cross")
            s_r = pl.sem("r")
            block = ctx.enter_context(nc.Block())
            TILES = 32

            def tiles(eng, body):
                for corner in range(4):
                    for p in range(2):
                        if corner == 0:
                            body(p, p, 0, corner, p)
                        else:
                            body(8 * corner + p, p, 4 * corner, corner, p)
                    with eng.Fori(1, 4) as j:
                        for p in range(2):
                            body(2 * j + (8 * corner + p), p, j + 4 * corner, corner, 2 * j + p)

            @block.sync
            def _(sp):
                sp.dma_start(diag[:], consts["diag8"]).then_inc(s_const, 16)

                def load(i, p, j, corner, m1):
                    if later(i):
                        sp.wait_ge(s_mm, i - 1)
                        load_weights(sp, p, corner, m1)

                tiles(sp, load)

            @block.scalar
            def _(act):
                act.wait_ge(s_zero, 2)

                def step(i, p, j, corner, m1):
                    if later(i):
                        act.wait_ge(s_mm, i - 1)
                    t = i
                    for q in range(2):
                        rows = slice(q * 64, q * 64 + 64)
                        src = S[rows, t] if isinstance(t, int) else S[rows, bass.ds(t, 1)].rearrange("q o f -> q (o f)")
                        act.activation(SZ[p][rows, :, q * 16:q * 16 + 16], src.rearrange("q (m f) -> q m f", f=16),
                                       ACT.Copy).then_inc(s_sz, 1)

                def out(i, p, j):
                    act.wait_ge(s_r, i + 1)
                    act.dma_start(modes_dram[bass.ds(i, 1)].rearrange("o p f -> (o p) f"), R[p][:]).then_inc(r_out[p], 16)

                step(0, 0, 0, 0, 0)

                def body(i, p, j, corner, m1):
                    if not (isinstance(i, int) and i == TILES - 1):
                        step(i + 1, 1 - p, j + p, corner, m1)
                    out(i, p, j)

                for i in range(2):
                    body(i, i, 0, 0, 0)
                with act.Fori(1, TILES // 2 - 1) as j:
                    body(2 * j, 0, j, 0, 0)
                    body(2 * j + 1, 1, j, 0, 0)
                for i in range(TILES - 2, TILES):
                    body(i, i % 2, i // 2, 0, 0)
                for p in range(2):
                    act.wait_ge(r_out[p], 16 * (TILES // 2))

            @block.gpsimd
            def _(pool):
                for p in range(2):
                    pool.memset(SZ[p][:], 0.0).then_inc(s_zero, 1)

            @block.tensor
            def _(pe):
                pe.wait_ge(s_zero, 2)

                def step(i, p, j):
                    pe.wait_ge(s_sz, 2 * i + 2)
                    pe.wait_ge(w_in[p], 64 * (j + 1))
                    if later(i):
                        pe.wait_ge(s_cross, i - 1)
                    wv = WT[p][:].rearrange("q o (m b a) -> q m a o b", m=M, a=2)
                    for m2 in range(M):
                        for odd in range(2):
                            at = (m2 // 4) * 512 + odd * 256
                            rows = m2 % 4 * 32
                            ins = pe.matmul(P[p][rows:rows + 32, at:at + 256], SZ[p][:, 2 * m2 + odd, :],
                                            wv[:, m2, odd], start=True, stop=True)
                    ins.then_inc(s_mm, 1)

                steps(pe, TILES, step)

            @block.vector
            def _(dve):
                dve.wait_ge(s_const, 16)

                def step(i, p, j):
                    dve.wait_ge(s_mm, i + 1)
                    if not (isinstance(i, int) and i == 0):
                        dve.wait_ge(s_r, i)
                    dve.tensor_tensor(cross[:].rearrange("q (n b) -> q n b", b=8),
                                      P[p][:, :].rearrange("q (n b) -> q n b", b=8),
                                      diag[:].unsqueeze(1).broadcast_to([128, 8 * C, 8]), ALU.mult).then_inc(s_cross, 1)
                    dve.wait_ge(s_cross, i + 1)
                    if later(i):
                        dve.wait_ge(r_out[p], 16 * j)
                    dve.tensor_reduce(R[p][:], cross[:].rearrange("q (n b) -> q n b", b=8), AX_X,
                                      ALU.add).then_inc(s_r, 1)

                steps(dve, TILES, step)

    with ExitStack() as ctx:
        pl = Places(nc, ctx, "B3")
        E1 = pl.sb("e1", [64, 2, 4, 8, 4, 64])
        ed = pl.sb("ed", [64, 128])
        P = [pl.ps(f"p{k}") for k in range(4)]
        Y = [pl.sb(f"y{k}", [128, 512]) for k in range(4)]
        s_in = pl.sem("in")
        s_mm = pl.sem("mm")
        s_y = pl.sem("y")
        y_out = [pl.sem(f"y_out{k}") for k in range(4)]
        block = ctx.enter_context(nc.Block())

        @block.sync
        def _(sp):
            sp.dma_start(ed[:], consts["ed0"]).then_inc(s_in, 16)
            src = modes_dram.rearrange("(hh dh m) (g q r b) f -> r dh q hh m g (b f)", hh=2, dh=2, g=4, q=2, r=2)
            for hh in range(2):
                for rdq in range(8):
                    r, dh, q = rdq // 4, rdq // 2 % 2, rdq % 2
                    lo = r * 32 + dh * 16 + q * 8
                    sp.dma_start(E1[lo:lo + 8, hh].rearrange("k g b m f -> k g (b m f)"),
                                 src[r, dh, q, hh]).then_inc(s_in, 16)
            for kh in range(KH):
                sp.wait_ge(s_y, kh + 1)
                sp.dma_start(images_dram[:, :, kh].rearrange("r d f -> (r d) f"), Y[kh % 4][:]).then_inc(y_out[kh % 4], 16)
            for k in range(4):
                sp.wait_ge(y_out[k], 16 * (KH // 4))

        @block.tensor
        def _(pe):
            pe.wait_ge(s_in, 16 * 17)
            for kh in range(KH):
                hh, m2 = divmod(kh, M)
                if kh >= 4:
                    pe.wait_ge(s_y, kh - 3)
                pe.matmul(P[kh % 4][:, :], ed[:, :], E1[:, hh, m2 % 4, :, m2 // 4, :],
                          start=True, stop=True).then_inc(s_mm, 1)

        @block.scalar
        def _(act):
            for kh in range(KH):
                act.wait_ge(s_mm, kh + 1)
                if kh >= 4:
                    act.wait_ge(y_out[kh % 4], 16 * (kh // 4))
                act.activation(Y[kh % 4][:], P[kh % 4][:, :], ACT.Copy).then_inc(s_y, 1)


def phase_images(nc, x, consts, params, images_dram, x3_dram, spectra3_dram):
    with ExitStack() as ctx:
        pl = Places(nc, ctx, "C")
        grid, spline_w, conv_w, conv_b = params
        KG = KNOTS // 4
        X = [pl.sb(f"x{p}", [128, ROW]) for p in range(2)]
        IM = [pl.sb(f"im{p}", [64, PAIR, 512]) for p in range(2)]
        AI = pl.sb("ai", [128, 4, 2, 128])
        XT = [pl.sb(f"xt{p}", [128, 16, 128]) for p in range(2)]
        TN = pl.sb("tn", [128, ROW])
        TT = pl.sb("tt", [128, 4, 4, 512])
        WK = [pl.sb(f"wk{b}", [128, ROW]) for b in range(3)]
        QK = [pl.sb(f"qk{b}", [128, ROW]) for b in range(4)]
        SG = pl.sb("sg", [128, 16, (H + 2) * PAIR], BF16)
        X3 = [pl.sb(f"x3{p}", [128, ROW]) for p in range(2)]
        XN3 = pl.sb("xn3", [128, ROW])
        hw = pl.sb("rows", [128, 4 * 512])
        Z = [pl.sb(f"z{p}", [128, G, PAIR * M3]) for p in range(2)]
        gh = pl.sb("gh", [64, 128])
        gw = pl.sb("gw", [128, 2, 512])
        fh = pl.sb("fh", [128, 128])
        fw = pl.sb("fw", [128, 2, 128])
        ident = pl.sb("ident", [128, 128])
        gavg = pl.sb("gavg", [128, 128])
        gsum = pl.sb("gsum", [128, 128])
        WC = pl.sb("wc", [128, 3, 6, C], BF16)
        BT = pl.sb("bt", [128, C])
        gk = pl.sb("gk", [128, KNOTS])
        ngk = pl.sb("ngk", [128, KNOTS])
        coef = pl.sb("coef", [128, KNOTS])
        scoef = pl.sb("scoef", [128, KNOTS])
        near = pl.sb("near", [128, KG])
        nnear = pl.sb("nnear", [128, KG])
        low = pl.sb("low", [128, KG])
        high = pl.sb("high", [128, KG])
        CW = pl.sb("cw", [128, KG, C])
        f0 = pl.sb("f0", [128, 1])
        BR = pl.sb("br", [128, 16 * C], BF16)
        ones = pl.sb("ones", [128, 128], BF16)
        rest = pl.sb("rest", [128, C])
        piece = pl.sb("piece", [128, C], BF16)
        PA = pl.ps("pa", 4 * 512)
        PB = [pl.ps(f"pb{k}") for k in range(2)]
        PF = pl.ps("pf")
        P_s = pl.ps("pstat")
        st = RowStats(pl, P_s)
        bn1 = pl.sb("bn1", [128, PAIR, 12])
        ms1 = pl.sb("ms1", [128, PAIR])
        vr1 = pl.sb("vr1", [128, PAIR])
        mean1 = pl.sb("mean1", [128, PAIR])
        dv1 = pl.sb("dv1", [128, PAIR, 4])
        dd1 = pl.sb("dd1", [128, PAIR, 4])
        sv1 = pl.sb("sv1", [128, PAIR, 4])
        ve1 = pl.sb("ve_ch", [128, PAIR])
        rstd1 = pl.sb("rs_ch", [128, PAIR])
        sum2 = pl.sb("sum2", [128, 4, PAIR])
        mean2 = pl.sb("mean2", [128, PAIR])
        bias4 = pl.sb("bias4", [128, 4 * C])
        wsp = pl.sb("wsp", [128, BASES])
        w4 = pl.sb("w4", [128, 4 * 9, C])
        wsum = pl.sb("wsum", [128, 9 * C])
        gaps = pl.sb("gaps", [128, KNOTS, KNOTS])
        prod = pl.sb("prod", [128, ORDER + 2, BASES])
        wspan = pl.sb("wspan", [128, BASES])
        shift = pl.sb("shift", [128, MID])
        mom = pl.sb("mom", [128, MID])
        pm1, pv1, pm2 = P_s[:, 160:162], P_s[:, 164:172], P_s[:, 176:184]

        s_const, s_param, s_set = pl.sem("const"), pl.sem("param"), pl.sem("set")
        s_ready0 = pl.sem("ready0")
        x_in = [pl.sem(f"x_in{p}") for p in range(2)]
        im_in = [pl.sem(f"im_in{p}") for p in range(2)]
        x3_out = [pl.sem(f"x3_out{p}") for p in range(2)]
        z_out = [pl.sem(f"z_out{p}") for p in range(2)]
        ring = pl.sem("ring")
        free = [pl.sem(f"free{k}") for k in range(3)]
        s_y = pl.sem("y")
        s_x1 = pl.sem("x1")
        s_bn1, s_ms1, s_vr1, s_pm1, s_mean1 = pl.sem("bn1s"), pl.sem("ms1s"), pl.sem("vr1s"), pl.sem("pm1s"), pl.sem("mean1s")
        s_dv1, s_dd1, s_sv1, s_pv1 = pl.sem("dv1s"), pl.sem("dd1s"), pl.sem("sv1s"), pl.sem("pv1s")
        s_ve1, s_rs1, s_tn = pl.sem("ve1s"), pl.sem("rs1s"), pl.sem("tns")
        t4_in = [pl.sem(f"t4_in{h}") for h in range(2)]
        s_w, s_q = pl.sem("ws"), pl.sem("qs")
        s_cube = [pl.sem(f"cube{e}") for e in range(2)]
        s_sq = pl.sem("sq")
        s_sum = pl.sem("sums")
        s_x2, s_pm2, s_mean2, s_sg = pl.sem("x2s"), pl.sem("pm2s"), pl.sem("mean2s"), pl.sem("sgs")
        s_t = pl.sem("turned_back")
        s_cv = pl.sem("cv")
        s_x3 = pl.sem("x3s")
        s_chain = pl.sem("chain")
        xv = x.rearrange("(n d) h w c -> n h d (w c)", d=PAIR)
        x3v = x3_dram.rearrange("(n d) h f -> n h d f", d=PAIR)
        block = ctx.enter_context(nc.Block())

        def first(i):
            return isinstance(i, int) and i == 0

        def last(i):
            return isinstance(i, int) and i == NP - 1

        def end(i):
            return isinstance(i, int) and i >= NP - 2

        def ring_use(base, half, l):
            return l % 2, half + l // 2, base + l + 1

        def back0_use(i, l):
            if isinstance(i, int) and i < 3:
                return ring_use(6 * i, 3 * i, l)
            return ring_use(12 * i - 18, 6 * i - 9, l)

        def turn_use(i, l):
            if isinstance(i, int) and i < 3:
                return ring_use(6 * i + 2, 3 * i + 1, l)
            return ring_use(12 * i - 16, 6 * i - 8, l)

        def back_use(i, l):
            if isinstance(i, int) and i >= NP - 3:
                return ring_use(12 * NP - 18 + 6 * (i - NP + 3), 6 * NP - 9 + 3 * (i - NP + 3), l)
            return ring_use(12 * i + 24, 6 * i + 12, l)

        TILES = 4 * KG
        POOL = (1, 4, 8, 10)

        def cube_made(eng, i, n):
            if n < 0:
                i, n = i - 1, n + TILES
            before = sum(m < n for m in POOL)
            if n in POOL:
                eng.wait_ge(s_cube[1], len(POOL) * i + before + 1)
            else:
                eng.wait_ge(s_cube[0], (TILES - len(POOL)) * i + n - before + 1)

        def cube(eng, i, n):
            g = n % KG
            eng.wait_ge(s_q, TILES * i + n + 1)
            q, w = QK[n % 4][:], WK[n % 3][:]
            if n in POOL:
                eng.tensor_tensor(q, w, q, ALU.mult).then_inc(s_cube[1], 1)
            else:
                eng.scalar_tensor_tensor(q, w, near[:, g:g + 1], q, ALU.subtract, ALU.mult).then_inc(s_cube[0], 1)

        @block.sync
        def _(sp):
            for dst, name in ((gh, "gh0"), (gw, "gw0"), (fh, "fh3"), (fw, "fw3"), (ident, "ident"),
                              (gavg, "gavg"), (gsum, "gsum"), (st.avg, "avg"), (st.var, "var")):
                sp.dma_start(dst[:], consts[name]).then_inc(s_const, 16)

            def load(i, p, j):
                if later(i):
                    sp.wait_ge(ring, turn_use(i - 2, 3)[2])
                sp.dma_start(X[p][:, :], xv[i]).then_inc(x_in[p], 16)
                for ri in range(2):
                    sp.dma_start(IM[p][ri * 32:ri * 32 + 32],
                                 images_dram[ri, bass.ds(i * PAIR, PAIR)].rearrange("d k f -> k d f")).then_inc(im_in[p], 16)

            def store_x3(i, p, j):
                sp.wait_ge(s_x3, 4 * i + 4)
                sp.dma_start(x3v[i], X3[p][:, :]).then_inc(x3_out[p], 16)

            def store_z(i, p, j):
                for l in range(2):
                    k, before, use = back_use(i, 4 + l)
                    sp.wait_ge(free[k], before + 1)
                for c2 in range(2):
                    for ri in range(2):
                        lo = c2 * 64 + ri * 32
                        sp.dma_start(spectra3_dram[:, :, c2, ri, bass.ds(i * PAIR * M3, PAIR * M3)],
                                     Z[p][lo:lo + 32]).then_inc(z_out[p], 16)

            def clamped(i, half):
                sp.wait_ge(s_w, TILES * i + TILES // 2 * (half + 1))

            def replicate(i):
                sp.wait_ge(s_tn, 2 * i + 2)
                for half in range(2):
                    if half == 1 and not first(i):
                        clamped(i - 1, 1)
                    for k in range(4):
                        for w4 in range(4):
                            sp.dma_start(TT[k * C:k * C + C, 2 * half:2 * half + 2, w4],
                                         TN[w4 * C:w4 * C + C, half * 1024:half * 1024 + 1024]
                                         .rearrange("q (b f) -> q b f", b=2)).then_inc(t4_in[half], 16)

            load(0, 0, 0)
            load(1, 1, 0)
            replicate(0)

            def step(i, p, j):
                if not end(i):
                    load(i + 2, p, j + 1)
                if not first(i):
                    store_x3(i - 1, 1 - p, j)
                if not last(i):
                    clamped(i, 0)
                if later(i):
                    store_z(i - 2, p, j)
                if not last(i):
                    replicate(i + 1)

            steps(sp, NP, step, peel=4)
            store_z(NP - 2, 0, 0)
            store_x3(NP - 1, 1, 0)
            store_z(NP - 1, 1, 0)
            for p in range(2):
                sp.wait_ge(x3_out[p], 16 * (NP // 2))
                sp.wait_ge(z_out[p], 64 * (NP // 2))

        @block.gpsimd
        def _(pool):
            pool.dma_start(gk[:], grid.rearrange("(o k) -> o k", o=1).broadcast_to([128, KNOTS])).then_inc(s_param, 16)
            pool.dma_start(bias4[:], conv_b.rearrange("m c -> (m c)").rearrange("(o k) -> o k", o=1)
                           .broadcast_to([128, 4 * C])).then_inc(s_param, 16)
            for g in range(4):
                rows = slice(g * C, g * C + C)
                pool.dma_start(wsp[rows], spline_w).then_inc(s_param, 16)
                pool.dma_start(w4[rows], conv_w.rearrange("m a b c o -> c (m a b) o")).then_inc(s_param, 16)
            pool.memset(SG[:], 0.0).then_inc(s_ready0, 1)
            pool.memset(WC[:], 0.0).then_inc(s_ready0, 1)
            pool.memset(BR[:], 0.0).then_inc(s_ready0, 1)
            pool.memset(ones[:], 1.0).then_inc(s_ready0, 1)
            pool.memset(st.mhalf[:, :, :], -0.5).then_inc(st.s_mh, 1)
            pool.wait_ge(st.s_mh, 1)

            def root1(i):
                pool.wait_ge(s_ve1, i + 1)
                if not first(i):
                    pool.wait_ge(s_tn, 2 * i)
                pool.tensor_tensor(rstd1[:], ve1[:], st.mhalf[:, 0, 0:PAIR], ALU.pow).then_inc(s_rs1, 1)

            def back(i, p, j):
                pool.wait_ge(st.s_mu, i + 1)
                if not first(i):
                    pool.wait_ge(ring, back_use(i - 1, 3)[2])
                center(pool, st, st.mu[:, :], X3[p][:, :], XN3[:, :])
                if later(i):
                    k, before, use = back_use(i - 2, 5)
                    pool.wait_ge(free[k], before + 1)
                row_stats_root(pool, st, i, p)

            root1(0)

            def step(i, p, j):
                for n in POOL:
                    cube(pool, i, n)
                    if n == 4 and not last(i):
                        root1(i + 1)
                if not first(i):
                    back(i - 1, 1 - p, j)

            steps(pool, NP, step)
            back(NP - 1, 1, 0)

        @block.scalar
        def _(act):
            def rows_back(i):
                for l in range(2):
                    k, before, use = back0_use(i, l)
                    act.wait_ge(ring, use)
                    if l == 0 and not first(i):
                        act.wait_ge(s_y, i)
                    act.activation(AI[:, 2 * l:2 * l + 2].rearrange("q g r n -> q (g r n)"), PB[k][:, :],
                                   ACT.Copy).then_inc(free[k], 1)

            def turned(i, p, j):
                for b in range(4):
                    k, before, use = turn_use(i, b)
                    act.wait_ge(ring, use)
                    if b == 0 and later(i):
                        act.wait_ge(s_t, 4 * (i - 1))
                        act.wait_ge(s_sg, 2 * (i - 1))
                    act.activation(XT[p][:, 4 * b:4 * b + 4].rearrange("q w n -> q (w n)"), PB[k][:, :],
                                   ACT.Copy).then_inc(free[k], 1)

            def rows3(i):
                for l in range(4):
                    k, before, use = back_use(i, l)
                    act.wait_ge(ring, use)
                    if l == 0 and not first(i):
                        act.wait_ge(ring, back_use(i - 1, 5)[2])
                    act.activation(hw[:, l * 512:l * 512 + 512], PB[k][:, :], ACT.Copy).then_inc(free[k], 1)

            act.wait_ge(s_set, 1)
            rows_back(0)
            turned(0, 0, 0)
            rows_back(1)

            def after_conv(i, p, j, banks):
                if later(i) and banks[0] == 0:
                    act.wait_ge(x3_out[p], 16 * j)
                    act.wait_ge(st.s_xn, i - 1)
                for b in banks:
                    act.wait_ge(s_cv, 4 * i + b + 1)
                    cols = slice(b * 512, b * 512 + 512)
                    act.activation(X3[p][:, cols], PA[:, cols], ACT.Copy).then_inc(s_x3, 1)

            def square(i, n):
                act.wait_ge(s_w, TILES * i + n + 1)
                if n >= 4 or not first(i):
                    act.wait_ge(s_sum, TILES * i + n - 3)
                q, w, minus = QK[n % 4][:], WK[n % 3][:], nnear[:, n % KG:n % KG + 1]
                if n in POOL:
                    k = len(POOL) * i + POOL.index(n) + 1
                    act.activation(q, w, ACT.Square, bias=minus).then_inc(s_sq, 1)
                    act.wait_ge(s_sq, k)
                    act.activation(w, w, ACT.Identity, bias=minus).then_inc(s_q, 1)
                else:
                    act.activation(q, w, ACT.Square, bias=minus).then_inc(s_q, 1)

            def step(i, p, j):
                for n in range(TILES):
                    square(i, n)
                    if n == 2 and not last(i):
                        turned(i + 1, 1 - p, j + p)
                    if n == 5 and not first(i):
                        after_conv(i - 1, 1 - p, j - 1 + p, (0, 1, 2, 3))
                    if n == 6 and later(i):
                        rows3(i - 2)
                    if n == 8 and not end(i):
                        rows_back(i + 2)

            steps(act, NP, step, peel=4)
            rows3(NP - 2)
            after_conv(NP - 1, 1, NP // 2 - 1, (0, 1, 2, 3))
            rows3(NP - 1)

        @block.vector
        def _(dve):
            chained = [0]

            def link(ins):
                chained[0] += 1
                ins.then_inc(s_chain, 1)
                dve.wait_ge(s_chain, chained[0])

            dve.wait_ge(s_param, 16 * 10)
            dve.wait_ge(s_const, 16 * 9)
            dve.wait_ge(s_ready0, 4)
            link(dve.tensor_scalar(w4[:], w4[:], 0.0, 4.0, ALU.is_ge, ALU.mult))
            w4m = w4[:].rearrange("q (m t) o -> q m (t o)", m=4)
            link(dve.tensor_reduce(wsum[:], w4m.rearrange("q m f -> q f m"), AX_X, ALU.add))
            link(dve.tensor_scalar(wsum[:], wsum[:], 8.0, None, ALU.subtract))
            taps = wsum[:].rearrange("q (a b o) -> q a b o", a=3, b=3)
            for g in range(4):
                rows = slice(g * C, g * C + C)
                for dw in range(3):
                    ins = dve.tensor_copy(WC[rows, :, g + 2 - dw, :], taps[rows, :, dw, :])
                    if (g, dw) == (3, 2):
                        link(ins)
            link(dve.tensor_reduce(BT[:], bias4[:].rearrange("q (m c) -> q c m", m=4), AX_X, ALU.add))
            for part in range(3):
                left_over = BT if part == 0 else rest
                link(dve.tensor_copy(piece[:], left_over[:]))
                rows = slice(part * C, part * C + 1)
                link(dve.tensor_copy(BR[rows, :].rearrange("q (w c) -> q w c", c=C),
                                     piece[rows, :].unsqueeze(1).broadcast_to([1, 16, C])))
                link(dve.tensor_tensor(rest[:], left_over[:], piece[:], ALU.subtract))
            link(dve.tensor_tensor(gaps[:], gk[:].unsqueeze(2).broadcast_to([128, KNOTS, KNOTS]),
                                   gk[:].unsqueeze(1).broadcast_to([128, KNOTS, KNOTS]), ALU.subtract))
            flat = gaps[:].rearrange("q a b -> q (a b)")

            def gap(a, b):
                lo = KNOTS * a + b
                return flat[:, lo:lo + (KNOTS + 1) * (BASES - 1) + 1:KNOTS + 1]

            for a in range(ORDER + 2):
                others = [b for b in range(ORDER + 2) if b != a]
                link(dve.tensor_tensor(prod[:, a], gap(a, others[0]), gap(a, others[1]), ALU.mult))
                for b in others[2:]:
                    link(dve.tensor_tensor(prod[:, a], prod[:, a], gap(a, b), ALU.mult))
            link(dve.reciprocal(prod[:], prod[:]))
            link(dve.tensor_tensor(wspan[:], gap(ORDER + 1, 0), wsp[:], ALU.mult))
            link(dve.tensor_tensor(prod[:], prod[:], wspan[:].unsqueeze(1).broadcast_to([128, ORDER + 2, BASES]), ALU.mult))
            link(dve.memset(coef[:], 0.0))
            for a in range(ORDER + 2):
                link(dve.tensor_tensor(coef[:, a:a + BASES], coef[:, a:a + BASES], prod[:, a], ALU.add))
            link(dve.memset(scoef[:], 0.0))
            link(dve.tensor_copy(scoef[:, 0:MID], coef[:, 0:MID]))
            link(dve.tensor_scalar(scoef[:, MID + 1:KNOTS], coef[:, MID + 1:KNOTS], -1.0, None, ALU.mult))
            link(dve.tensor_scalar(shift[:], gk[:, 0:MID], gk[:, MID:MID + 1], None, ALU.subtract))
            link(dve.tensor_copy(mom[:], coef[:, 0:MID]))
            for n in range(ORDER):
                link(dve.tensor_tensor(mom[:], mom[:], shift[:], ALU.mult))
            link(dve.tensor_reduce(f0[:], mom[:], AX_X, ALU.add))
            for k in range(4):
                rows = slice(k * C, k * C + C)
                link(dve.tensor_copy(near[rows], gk[rows, k::4]))
                for g in range(KG):
                    link(dve.tensor_scalar(CW[rows, g], ident[rows, rows], scoef[rows, 4 * g + k:4 * g + k + 1],
                                           None, ALU.mult))
            link(dve.tensor_scalar(nnear[:], near[:], -1.0, None, ALU.mult))
            link(dve.tensor_scalar(low[:], near[:], gk[:, MID:MID + 1], None, ALU.min))
            dve.tensor_scalar(high[:], near[:], gk[:, MID:MID + 1], None, ALU.max).then_inc(s_set, 1)
            dve.wait_ge(s_set, 1)

            def add_x1(i, p, j):
                dve.wait_ge(s_y, i + 1)
                dve.wait_ge(x_in[p], 16 * (j + 1))
                xg = X[p][:, :].rearrange("q (w o g) -> q g w o", o=8, g=4)
                dve.tensor_tensor(xg, PA[:, :].rearrange("q (g w o) -> q g w o", g=4, o=8), xg,
                                  ALU.add).then_inc(s_x1, 1)

            def normalise(i, p, j):
                for b in range(4):
                    k, before, use = turn_use(i, b)
                    dve.wait_ge(free[k], before + 1)
                xi = XT[p][:].rearrange("q w (h d) -> q d w h", d=PAIR)
                for d2 in range(PAIR):
                    for half in range(2):
                        ins = dve.bn_stats(bn1[:, d2, half * 6:half * 6 + 6], xi[:, d2, half * 8:half * 8 + 8])
                ins.then_inc(s_bn1, 1)
                dve.wait_ge(s_bn1, i + 1)
                parts = bn1[:].rearrange("q d (n s) -> q d n s", s=3)
                dve.tensor_reduce(ms1[:], parts[:, :, :, 1], AX_X, ALU.add).then_inc(s_ms1, 1)

            def deviations(i):
                parts = bn1[:].rearrange("q d (n s) -> q d n s", s=3)
                dve.wait_ge(s_pm1, i + 1)
                dve.tensor_copy(mean1[:], pm1).then_inc(s_mean1, 1)
                dve.wait_ge(s_mean1, i + 1)
                dve.tensor_tensor(dv1[:], parts[:, :, :, 1], mean1[:].unsqueeze(2).broadcast_to([128, PAIR, 4]),
                                  ALU.subtract).then_inc(s_dv1, 1)
                dve.wait_ge(s_dv1, i + 1)
                dve.scalar_tensor_tensor(dd1[:], dv1[:], float(H * W // 16), dv1[:], ALU.mult,
                                         ALU.mult).then_inc(s_dd1, 1)
                dve.wait_ge(s_dd1, i + 1)
                dve.tensor_tensor(sv1[:], dd1[:], parts[:, :, :, 2], ALU.add).then_inc(s_sv1, 1)

            def variance1(i):
                dve.wait_ge(s_pv1, i + 1)
                dve.tensor_reduce(vr1[:], pv1.rearrange("q (d n) -> q d n", d=PAIR), AX_X, ALU.add).then_inc(s_vr1, 1)
                dve.wait_ge(s_vr1, i + 1)
                dve.tensor_scalar(ve1[:], vr1[:], EPS, None, ALU.add).then_inc(s_ve1, 1)

            def scale_in(i, p, j):
                dve.wait_ge(s_rs1, i + 1)
                if not first(i):
                    for half in range(2):
                        dve.wait_ge(t4_in[half], 256 * i)
                xi = XT[p][:].rearrange("q w (h d) -> q d w h", d=PAIR)
                ti = TN[:].rearrange("q (w h d) -> q d w h", h=H, d=PAIR)
                for d2 in range(PAIR):
                    dve.tensor_scalar(ti[:, d2], xi[:, d2], mean1[:, d2:d2 + 1], rstd1[:, d2:d2 + 1],
                                      ALU.subtract, ALU.mult).then_inc(s_tn, 1)

            def spectra(i, p, j):
                if later(i):
                    dve.wait_ge(z_out[p], 64 * j)
                dve.wait_ge(st.s_rstd, i + 1)
                for l in range(2):
                    k, before, use = back_use(i, 4 + l)
                    dve.wait_ge(ring, use)
                    dve.tensor_tensor(Z[p][:, l * 8:l * 8 + 8].rearrange("q g (d h) -> q g d h", d=PAIR),
                                      PB[k][:, :].rearrange("q (g d h) -> q g d h", g=8, d=PAIR),
                                      st.rstd[p][:, :, l * 8:l * 8 + 8].rearrange("q d g -> q g d").unsqueeze(3)
                                      .broadcast_to([128, 8, PAIR, M3]), ALU.mult).then_inc(free[k], 1)

            def clamp(i, n):
                b, g = n // KG, n % KG
                if n % (2 * KG) == 0:
                    dve.wait_ge(t4_in[n // (2 * KG)], 256 * (i + 1))
                if n >= 3 or not first(i):
                    cube_made(dve, i, n - 3)
                dve.tensor_scalar(WK[n % 3][:], TT[:, b].rearrange("q w f -> q (w f)"), low[:, g:g + 1], high[:, g:g + 1],
                                  ALU.max, ALU.min).then_inc(s_w, 1)

            def add_spline(i, p, b):
                dve.wait_ge(s_sum, TILES * i + KG * b + KG)
                xi = XT[p][:, 4 * b:4 * b + 4].rearrange("q w (h d) -> q d w h", d=PAIR)
                fi = PF[:, :].rearrange("q (w h d) -> q d w h", h=H, d=PAIR)
                for d2 in range(PAIR):
                    dve.scalar_tensor_tensor(xi[:, d2], fi[:, d2], f0[:], xi[:, d2], ALU.add, ALU.add,
                                             accum_out=sum2[:, b, d2:d2 + 1]).then_inc(s_x2, 1)

            def signs(i, p, j):
                dve.wait_ge(s_pm2, i + 1)
                dve.tensor_reduce(mean2[:], pm2.rearrange("q (b d) -> q d b", d=PAIR), AX_X, ALU.add).then_inc(s_mean2, 1)
                dve.wait_ge(s_mean2, i + 1)
                if not first(i):
                    dve.wait_ge(s_cv, 4 * i)
                for d2 in range(PAIR):
                    dve.tensor_scalar(SG[:, :, PAIR + d2:PAIR + PAIR * H + d2:PAIR], XT[p][:, :, d2::PAIR],
                                      mean2[:, d2:d2 + 1], 0.5, ALU.is_ge, ALU.subtract).then_inc(s_sg, 1)

            def back_stats(i, p):
                dve.wait_ge(s_x3, 4 * i + 4)
                row_stats_start(dve, st, i, X3[p][:, :])

            add_x1(0, 0, 0)
            normalise(0, 0, 0)
            deviations(0)
            variance1(0)
            scale_in(0, 0, 0)
            add_x1(1, 1, 0)

            def step(i, p, j):
                q, jf, jb = 1 - p, j + p, j - 1 + p
                clamp(i, 0)
                clamp(i, 1)
                clamp(i, 2)
                if not first(i):
                    add_spline(i - 1, q, 3)
                for n in range(TILES):
                    if n not in POOL:
                        cube(dve, i, n)
                        if n - 1 in POOL and n + 2 < TILES:
                            clamp(i, n + 2)
                        if n + 3 < TILES:
                            clamp(i, n + 3)
                    if n == 0 and not first(i):
                        signs(i - 1, q, jb)
                    if n == 2 and not last(i):
                        normalise(i + 1, q, jf)
                    if n == 3 and not last(i):
                        deviations(i + 1)
                    if n in (3, 6, 9):
                        add_spline(i, p, n // KG - 1)
                    if n == 4 and not last(i):
                        variance1(i + 1)
                    if n == 6 and later(i):
                        spectra(i - 2, p, j - 1)
                    if n == 5 and not last(i):
                        scale_in(i + 1, q, jf)
                    if n == 10 and not end(i):
                        add_x1(i + 2, p, j + 1)
                    if n == 8 and not first(i):
                        back_stats(i - 1, q)
                    if n == 9 and not first(i):
                        row_stats_middle(dve, st, i - 1)
                    if n == 10 and not first(i):
                        row_stats_end(dve, st, i - 1, q)

            steps(dve, NP, step, peel=4)
            add_spline(NP - 1, 1, 3)
            spectra(NP - 2, 0, NP // 2 - 1)
            signs(NP - 1, 1, NP // 2 - 1)
            back_stats(NP - 1, 1)
            row_stats_middle(dve, st, NP - 1)
            row_stats_end(dve, st, NP - 1, 1)
            spectra(NP - 1, 1, NP // 2 - 1)

        @block.tensor
        def _(pe):
            pe.wait_ge(s_const, 16 * 9)
            pe.wait_ge(s_set, 1)

            def back0(i, p, j):
                pe.wait_ge(im_in[p], 32 * (j + 1))
                for l in range(2):
                    k, before, use = back0_use(i, l)
                    if not (isinstance(before, int) and before == 0):
                        pe.wait_ge(free[k], before)
                    bank = PB[k][:, :].rearrange("q (g r h d) -> q g d r h", g=2, r=2, d=PAIR)
                    for g in range(2):
                        for d2 in range(PAIR):
                            ins = pe.matmul(bank[:, g, d2], IM[p][:, d2, 2 * l + g::4], gh[:, :],
                                            start=True, stop=True)
                    ins.then_inc(ring, 1)

            def back0_w(i, banks):
                if banks[0] == 0:
                    for l in range(2):
                        k, before, use = back0_use(i, l)
                        pe.wait_ge(free[k], before + 1)
                    if not first(i):
                        pe.wait_ge(s_x1, i)
                for g in banks:
                    if not isinstance(i, int) or i >= 3:
                        pe.wait_ge(s_x3, 4 * (i - 3) + g + 1)
                    for ri in range(2):
                        ins = pe.matmul(PA[:, g * 512:g * 512 + 512], AI[:, g, ri], gw[:, ri],
                                        start=(ri == 0), stop=(ri == 1))
                if banks[-1] == 3:
                    ins.then_inc(s_y, 1)

            def turn(i, p, j):
                pe.wait_ge(s_x1, i + 1)
                for b in range(4):
                    k, before, use = turn_use(i, b)
                    if not (isinstance(before, int) and before == 0):
                        pe.wait_ge(free[k], before)
                    for n in range(4):
                        at = (4 * b + n) * 128
                        ins = pe.transpose(PB[k][:, n * 128:n * 128 + 128], X[p][:, at:at + 128], ident[:, :])
                    ins.then_inc(ring, 1)

            def mean1_tensor(i):
                pe.wait_ge(s_ms1, i + 1)
                pe.matmul(pm1, gavg[:, :], ms1[:], start=True, stop=True).then_inc(s_pm1, 1)

            def variance1_tensor(i):
                pe.wait_ge(s_sv1, i + 1)
                pe.matmul(pv1, gsum[:, :], sv1[:].rearrange("q d n -> q (d n)"), start=True, stop=True).then_inc(s_pv1, 1)

            def conv(i, banks):
                if banks[0] == 0:
                    pe.wait_ge(s_sg, 2 * i + 2)
                for b in banks:
                    lo = b * 512
                    for blk in range(max(4 * b - 1, 0), min(4 * b + 5, 16)):
                        c0 = max((4 * blk - 1) * C, lo)
                        c1 = min((4 * blk + 5) * C, lo + 512)
                        off = (4 * blk - 1) * C
                        for dh in range(3):
                            ins = pe.matmul(PA[:, c0:c1], SG[:, blk, PAIR * dh:PAIR * dh + 128],
                                            WC[:, dh].rearrange("q w c -> q (w c)")[:, c0 - off:c1 - off],
                                            start=False, stop=False, skip_group_check=True)
                    pe.matmul(PA[:, lo:lo + 512], ones[:, :], BR[:, :], start=False, stop=True,
                              skip_group_check=True).then_inc(s_cv, 1)

            def forward3(i):
                pe.wait_ge(st.s_xn, i + 1)
                for l in range(4):
                    k, before, use = back_use(i, l)
                    pe.wait_ge(free[k], before)
                    for n in range(4):
                        at = (4 * l + n) * 128
                        ins = pe.matmul(PB[k][:, n * 128:n * 128 + 128], XN3[:, at:at + 128], fh[:, :],
                                        start=True, stop=True)
                    ins.then_inc(ring, 1)

            def forward3_w(i):
                for l in range(2):
                    k, before, use = back_use(i, 4 + l)
                    pe.wait_ge(free[k], before)
                    for m in range(2):
                        kk, bb, uu = back_use(i, 2 * l + m)
                        pe.wait_ge(free[kk], bb + 1)
                    hv = hw[:].rearrange("q (g r n) -> q r g n", g=G, r=2)
                    for ri in range(2):
                        ins = pe.matmul(PB[k][:, :], fw[:, ri], hv[:, ri, l * 8:l * 8 + 8],
                                        start=(ri == 0), stop=(ri == 1))
                    ins.then_inc(ring, 1)

            def turn_back(i, p, b):
                pe.wait_ge(s_x2, 8 * i + 2 * b + 2)
                pe.wait_ge(s_x1, NP if end(i) else i + 3)
                for n in range(4):
                    at = (4 * b + n) * 128
                    ins = pe.matmul(PA[:, at:at + 128], XT[p][:, 4 * b + n], ident[:, :],
                                    start=(n == 0), stop=False, skip_group_check=True)
                ins.then_inc(s_t, 1)

            def add_up(i, n):
                g = n % KG
                cube_made(pe, i, n)
                if g == 0 and (n > 0 or not first(i)):
                    pe.wait_ge(s_x2, 8 * i + 2 * (n // KG))
                for w4 in range(4):
                    ins = pe.matmul(PF[w4 * C:w4 * C + C, :], CW[:, g], QK[n % 4][:, w4 * 512:w4 * 512 + 512],
                                    start=(g == 0), stop=(g == KG - 1), tile_position=(0, w4 * C))
                ins.then_inc(s_sum, 1)

            def mean2_tensor(i):
                pe.wait_ge(s_x2, 8 * i + 8)
                pe.matmul(pm2, gsum[:, :], sum2[:].rearrange("q b d -> q (b d)"), start=True, stop=True).then_inc(s_pm2, 1)

            back0(0, 0, 0)
            back0_w(0, (0, 1, 2, 3))
            turn(0, 0, 0)
            mean1_tensor(0)
            variance1_tensor(0)
            back0(1, 1, 0)
            back0_w(1, (0, 1, 2, 3))

            def step(i, p, j):
                q, jf = 1 - p, j + p
                if not first(i):
                    mean2_tensor(i - 1)
                    turn_back(i - 1, q, 3)
                for n in range(TILES):
                    add_up(i, n)
                    if n == 0 and not last(i):
                        turn(i + 1, q, jf)
                    if n in (0, 1) and not first(i):
                        conv(i - 1, (2 * n, 2 * n + 1))
                    if n == 1 and not last(i):
                        mean1_tensor(i + 1)
                    if n == 2 and not last(i):
                        variance1_tensor(i + 1)
                    if n == 3 and later(i):
                        forward3(i - 2)
                    if n == 5 and later(i):
                        forward3_w(i - 2)
                    if n == 5 and not end(i):
                        back0(i + 2, p, j + 1)
                    if n == 8 and not first(i):
                        row_mean_tensor(pe, st, i - 1)
                    if n in (7, 8) and not end(i):
                        back0_w(i + 2, (0, 1) if n == 7 else (2, 3))
                    if n in (10, 11):
                        for b in {10: (0, 1), 11: (2,)}[n]:
                            turn_back(i, p, b)
                    if n == 9 and not first(i):
                        row_variance_tensor(pe, st, i - 1)

            steps(pe, NP, step)
            mean2_tensor(NP - 1)
            forward3(NP - 2)
            forward3_w(NP - 2)
            turn_back(NP - 1, 1, 3)
            conv(NP - 1, (0, 1, 2, 3))
            row_mean_tensor(pe, st, NP - 1)
            row_variance_tensor(pe, st, NP - 1)
            forward3(NP - 1)
            forward3_w(NP - 1)


def phase_modes3(nc, consts, conv_w, spectra3_dram, mixed_dram):
    with ExitStack() as ctx:
        pl = Places(nc, ctx, "D")
        XD = [pl.sb(f"x{p}", [128, 2 * D, M3]) for p in range(2)]
        WB = [pl.sb(f"w{p}", [128, M3, 4, C]) for p in range(2)]
        GS = [pl.sb(f"g{p}", [128, M3, 128]) for p in range(2)]
        P = [pl.ps(f"p{b}") for b in range(8)]
        s_zero = pl.sem("zero")
        x_in = [pl.sem(f"x_in{p}") for p in range(2)]
        w_in = [pl.sem(f"w_in{p}") for p in range(2)]
        g_out = [pl.sem(f"g_out{p}") for p in range(2)]
        s_mm = pl.sem("mm")
        s_g = [pl.sem(f"g{e}") for e in range(2)]
        TURNS = M3 // 4
        xv = spectra3_dram.rearrange("(t k) g c r f -> t (k g c) r f", k=4)
        wv = conv_w.rearrange("h (t k) c o -> t k c h o", k=4)
        block = ctx.enter_context(nc.Block())

        def copy_out(eng, copy, share):
            def step(i, p, j):
                if later(i):
                    eng.wait_ge(g_out[p], 16 * j)
                for b in range(share, 8, 2):
                    eng.wait_ge(s_mm, 8 * i + b + 1)
                    copy(GS[p][:, 4 * b:4 * b + 4].rearrange("q h n -> q (h n)"), P[b][:, :]).then_inc(s_g[share], 1)

            steps(eng, TURNS, step)

        @block.sync
        def _(sp):
            sp.wait_ge(s_zero, 2)

            def load(i, p, j):
                if later(i):
                    sp.wait_ge(s_mm, 8 * (i - 1))
                sp.dma_start(XD[p][:].rearrange("q (r d) h -> q r (d h)", r=2), xv[i]).then_inc(x_in[p], 16)
                for k in range(4):
                    sp.dma_start(WB[p][k * C:k * C + C, :, k, :], wv[i, k]).then_inc(w_in[p], 16)

            steps(sp, TURNS, load)

        @block.gpsimd
        def _(pool):
            for p in range(2):
                pool.memset(WB[p][:], 0.0).then_inc(s_zero, 1)
            dst = mixed_dram.rearrange("r d h (t n) -> t (r d) h n", n=128)

            def store(i, p, j):
                for e in range(2):
                    pool.wait_ge(s_g[e], 4 * i + 4)
                pool.dma_start(dst[i], GS[p][:]).then_inc(g_out[p], 16)

            steps(pool, TURNS, store)
            for p in range(2):
                pool.wait_ge(g_out[p], 16 * (TURNS // 2))

        @block.vector
        def _(dve):
            copy_out(dve, lambda d, s: dve.tensor_copy(d, s), 0)

        @block.scalar
        def _(act):
            copy_out(act, lambda d, s: act.activation(d, s, ACT.Copy), 1)

        @block.tensor
        def _(pe):
            def step(i, p, j):
                pe.wait_ge(x_in[p], 16 * (j + 1))
                pe.wait_ge(w_in[p], 64 * (j + 1))
                for h in range(M3):
                    b = h // 4
                    if h % 4 == 0 and not (isinstance(i, int) and i == 0):
                        pe.wait_ge(s_g[b % 2], 4 * (i - 1) + b // 2 + 1)
                    ins = pe.matmul(P[b][:, h % 4 * 128:h % 4 * 128 + 128], XD[p][:, :, h],
                                    WB[p][:, h].rearrange("q k o -> q (k o)"), start=True, stop=True)
                    if h % 4 == 3:
                        ins.then_inc(s_mm, 1)

            steps(pe, TURNS, step)


def phase_back3(nc, consts, mixed_dram, x3_dram, out):
    with ExitStack() as ctx:
        pl = Places(nc, ctx, "E")
        X = [pl.sb(f"x{p}", [128, ROW]) for p in range(2)]
        O = [pl.sb(f"o{p}", [128, ROW]) for p in range(2)]
        IM = [pl.sb(f"im{p}", [64, PAIR, M3 * C]) for p in range(2)]
        AI = [pl.sb(f"ai{p}", [128, 8, 2, 128]) for p in range(2)]
        gh = pl.sb("gh", [64, 128])
        gw = pl.sb("gw", [128, 2, 256])
        PR = [pl.ps(f"pr{b}") for b in range(4)]
        PY = [pl.ps(f"py{b}") for b in range(4)]
        s_const = pl.sem("const")
        x_in = [pl.sem(f"x_in{p}") for p in range(2)]
        im_in = [pl.sem(f"im_in{p}") for p in range(2)]
        o_out = [pl.sem(f"o_out{p}") for p in range(2)]
        s_r = pl.sem("r")
        s_ai = pl.sem("ai")
        s_y = pl.sem("y")
        s_o = pl.sem("o")
        xv = x3_dram.rearrange("(n d) h f -> n h d f", d=PAIR)
        ov = out.rearrange("(n d) h w c -> n h d (w c)", d=PAIR)
        block = ctx.enter_context(nc.Block())

        @block.sync
        def _(sp):
            sp.dma_start(gh[:], consts["gh3"]).then_inc(s_const, 16)
            sp.dma_start(gw[:], consts["gw3"]).then_inc(s_const, 16)

            def load(i, p, j):
                if later(i):
                    sp.wait_ge(s_r, 4 * (i - 1))
                for ri in range(2):
                    sp.dma_start(IM[p][ri * 32:ri * 32 + 32],
                                 mixed_dram[ri, bass.ds(i * PAIR, PAIR)].rearrange("d k f -> k d f")).then_inc(im_in[p], 16)
                if later(i):
                    sp.wait_ge(s_o, 4 * (i - 1))
                sp.dma_start(X[p][:, :], xv[i]).then_inc(x_in[p], 16)

            steps(sp, NP, load)

        @block.scalar
        def _(act):
            def step(i, p, j):
                for b in range(4):
                    act.wait_ge(s_r, 4 * i + b + 1)
                    if b == 0 and later(i):
                        act.wait_ge(s_y, 4 * (i - 1))
                    act.activation(AI[p][:, 2 * b:2 * b + 2].rearrange("q g r n -> q (g r n)"), PR[b][:, :],
                                   ACT.Copy).then_inc(s_ai, 1)

            steps(act, NP, step)

        @block.gpsimd
        def _(pool):
            def store(i, p, j):
                pool.wait_ge(s_o, 4 * i + 4)
                pool.dma_start(ov[i], O[p][:, :]).then_inc(o_out[p], 16)

            steps(pool, NP, store)
            for p in range(2):
                pool.wait_ge(o_out[p], 16 * (NP // 2))

        @block.vector
        def _(dve):
            def step(i, p, j):
                dve.wait_ge(x_in[p], 16 * (j + 1))
                if later(i):
                    dve.wait_ge(o_out[p], 16 * j)
                xg = X[p][:, :].rearrange("q (w o g) -> q g w o", o=4, g=8)
                og = O[p][:, :].rearrange("q (w o g) -> q g w o", o=4, g=8)
                for b in range(4):
                    dve.wait_ge(s_y, 4 * i + b + 1)
                    dve.tensor_tensor(og[:, 2 * b:2 * b + 2], PY[b][:, :].rearrange("q (g w o) -> q g w o", g=2, o=4),
                                      xg[:, 2 * b:2 * b + 2], ALU.add).then_inc(s_o, 1)

            steps(dve, NP, step)

        @block.tensor
        def _(pe):
            pe.wait_ge(s_const, 32)

            def rows(i, p, j):
                pe.wait_ge(im_in[p], 32 * (j + 1))
                for b in range(4):
                    if not (isinstance(i, int) and i == 0):
                        pe.wait_ge(s_ai, 4 * (i - 1) + b + 1)
                    bank = PR[b][:, :].rearrange("q (g r h d) -> q g d r h", g=2, r=2, d=PAIR)
                    for g in range(2):
                        for d2 in range(PAIR):
                            ins = pe.matmul(bank[:, g, d2], IM[p][:, d2, 2 * b + g::8], gh[:, :],
                                            start=True, stop=True)
                    ins.then_inc(s_r, 1)

            def cols(i, p, j):
                for b in range(4):
                    pe.wait_ge(s_ai, 4 * i + b + 1)
                    if not (isinstance(i, int) and i == 0):
                        pe.wait_ge(s_o, 4 * (i - 1) + b + 1)
                    for g in range(2):
                        for ri in range(2):
                            ins = pe.matmul(PY[b][:, g * 256:g * 256 + 256], AI[p][:, 2 * b + g, ri], gw[:, ri],
                                            start=(ri == 0), stop=(ri == 1))
                    ins.then_inc(s_y, 1)

            def step(i, p, j):
                if not (isinstance(i, int) and i == NP - 1):
                    rows(i + 1, 1 - p, j + p)
                cols(i, p, j)

            rows(0, 0, 0)
            steps(pe, NP, step)


def tables():
    import numpy as np

    kd = np.r_[0:M, -M:0]
    n = np.arange(D)
    full = 2 * D - 1
    two, sc = np.eye(2), 1.0 / full ** 1.5

    def cis(k, n, period):
        a = 2 * np.pi * np.outer(k, n) / period
        return np.cos(a), np.sin(a)

    def forward_rows(cos, sin, scale=1.0):
        return scale * np.einsum("de,rkh->hdrek", two, np.stack([cos, -sin])).reshape(128, -1)

    def inverse_rows(cos, sin):
        return np.block([[cos, sin], [-sin, cos]])

    c, s = cis(kd, n, full)
    out = {"fh0": forward_rows(c, s, sc), "gh0": inverse_rows(c, s), "ed0": inverse_rows(c, s)}
    fre = np.concatenate([c.T, s.T])
    fim = np.concatenate([-s.T, c.T])
    roles = np.stack([np.stack([fre, fim], -1), np.stack([-fim, fre], -1)], 1)
    roles = roles.reshape(128, 2, 2, 2, 8, 2).transpose(0, 1, 3, 2, 4, 5)
    out["fd0"] = roles.reshape(128, 128)
    cw, sw = cis(np.arange(KW), n, full)
    out["fw0"] = np.stack([
        np.einsum("ce,rkw->cwrek", two, np.stack([cw, -sw])).reshape(128, 64),
        np.einsum("ce,rkw->cwrek", two, np.stack([sw, cw])).reshape(128, 64)], 1)
    weight = np.where(np.arange(KW) == 0, 1.0, 2.0)[:, None] * sc
    out["gw0"] = np.stack([np.einsum("kw,oq->kowq", weight * t, np.eye(8)).reshape(128, 512)
                           for t in (cw, -sw)], 1)
    k3 = np.arange(M3)
    c3, s3 = cis(k3, n, H)
    out["fh3"] = forward_rows(c3, s3)
    out["gh3"] = inverse_rows(c3, s3)
    out["fw3"] = np.stack([
        np.einsum("ce,rkw->cwerk", two, np.stack([c3, -s3])).reshape(128, 128),
        np.einsum("ce,rkw->cwerk", two, np.stack([s3, c3])).reshape(128, 128)], 1)
    weight = np.where(k3 == 0, 1.0, 2.0)[:, None] / (H * W)
    out["gw3"] = np.stack([np.einsum("kw,oq->kowq", weight * t, np.eye(4)).reshape(128, 256)
                           for t in (c3, -s3)], 1)
    image = np.kron(np.ones((64, 64)), np.eye(2))
    out["avg"] = image / 128
    out["var"] = np.stack([np.repeat((np.arange(128) % 2 == d)[:, None], 128, 1) / (H * W * 2.0)
                           for d in range(2)], 1)
    group = (np.arange(128) % 32) // 2
    same = (group[:, None] == group[None, :]).astype(float)
    out["gavg"] = same / 32
    out["gsum"] = same / (H * W * 2.0)
    out["ident"] = np.eye(128)
    out["diag8"] = (np.arange(128)[:, None] % 8 == np.arange(8)[None, :]).astype(float)
    return {k: np.ascontiguousarray(v, dtype=np.float32) for k, v in out.items()}


def build(nc, args, consts, out):

    def scratch(name, shape):
        return nc.dram_tensor(name, shape, F32).ap()

    spectra = scratch("spectra", [2, D, 2, 32, 256])
    modes = scratch("modes", [32, 128, 256])
    images = scratch("images", [2, D, KH, KW * C])
    x3 = scratch("x3", [D, H, ROW])
    spectra3 = scratch("spectra3", [M3, G, 2, 2, D * M3])
    mixed = scratch("mixed", [2, D, M3, M3 * C])
    weights = [(args[f"L0_conv_w{n}r"], args[f"L0_conv_w{n}i"]) for n in range(1, 5)]
    params = (args["L1_conv_grid"], args["L1_conv_W"], args["L2_conv_W"], args["L2_conv_b"])
    phase_forward(nc, args["x"], consts, spectra)
    phase_depth(nc, consts, spectra, weights, modes, images)
    phase_images(nc, args["x"], consts, params, images, x3, spectra3)
    phase_modes3(nc, consts, args["L3_conv_W"], spectra3, mixed)
    phase_back3(nc, consts, mixed, x3, out)


_INS = ["x"] + [f"L0_conv_w{n}{part}" for n in range(1, 5) for part in "ri"] + [
    "L1_conv_grid", "L1_conv_W", "L2_conv_W", "L2_conv_b", "L3_conv_W"]


def kernel(**inputs):
    import numpy as np
    import concourse.bacc as bacc
    from concourse.bass_utils import run_bass_kernel_spmd

    nc = bacc.Bacc("TRN2", target_bir_lowering=False, num_devices=1)
    arrays, args, consts = {}, {}, {}
    for name in _INS:
        arrays[f"in_{name}"] = np.ascontiguousarray(inputs[name])
        args[name] = nc.dram_tensor(f"in_{name}", arrays[f"in_{name}"].shape, F32, kind="ExternalInput").ap()
    for name, table in tables().items():
        arrays[f"table_{name}"] = table
        consts[name] = nc.dram_tensor(f"table_{name}", table.shape, F32, kind="ExternalInput").ap()
    out = nc.dram_tensor("out_y", (D, H, W, C), F32, kind="ExternalOutput").ap()
    build(nc, args, consts, out)
    r = run_bass_kernel_spmd(nc, [arrays], core_ids=[0])
    return r.results[0]["out_y"]
```
